# Optimizing a Trainium2 kernel written in Bass

```python
import numpy as np
import jax
import jax.numpy as jnp

def _softmax(x, axis=-1):
    return jax.nn.softmax(x, axis=axis)

def _gelu(x):
    return jax.nn.gelu(x, approximate=True)

def _silu(x):
    return jax.nn.silu(x)

def _sigmoid(x):
    return jax.nn.sigmoid(x)

def _layernorm(x, axis=-1, eps=1e-05):
    m = jnp.mean(x, axis=axis, keepdims=True)
    v = jnp.var(x, axis=axis, keepdims=True)
    return (x - m) / jnp.sqrt(v + eps)

def _scatter_add(tgt, idx, src, axis=0):
    return tgt.at[idx].add(src)

def _segment_sum(src, seg, n):
    return jax.ops.segment_sum(src, seg, n)
kernel_name = 'mk_prb_d1_jaxref_r8_4614e4'

def setup_inputs(seed: int=0):
    np.random.seed(seed)
    _w = jnp.asarray

    def _L0_attn_setup():
        import jax, jax.numpy as jnp
        import numpy as np
        B, L, HID = (8, 1025, 128)
        H, KV, DH = (16, 4, 64)
        EPS = 1e-06
        ROPE_BASE = 10000.0

        def _rms_norm(x, w):
            var = jnp.mean(jnp.square(x), axis=-1, keepdims=True)
            return x * jax.lax.rsqrt(var + EPS) * w

        def _rotate_half(x):
            x1, x2 = jnp.split(x, 2, axis=-1)
            return jnp.concatenate([-x2, x1], axis=-1)

        def _rope_cache(seq_len, dim):
            inv_freq = 1.0 / ROPE_BASE ** (jnp.arange(0, dim, 2, dtype=jnp.float32) / dim)
            pos = jnp.arange(seq_len, dtype=jnp.float32)
            freqs = pos[:, None] * inv_freq[None, :]
            emb = jnp.concatenate([freqs, freqs], axis=-1)
            return (jnp.cos(emb), jnp.sin(emb))
        key = jax.random.key(seed)
        ks = jax.random.split(key, 5)
        s_in = 1.0
        s_q = float(np.sqrt(2.0 / (HID + H * DH)))
        s_kv = float(np.sqrt(2.0 / (HID + KV * DH)))
        s_o = float(np.sqrt(2.0 / (H * DH + HID)) / np.sqrt(2.0))
        return {'inputs': jax.random.normal(ks[0], (B, L, HID), jnp.float32) * s_in, 'Wq': jax.random.normal(ks[1], (H * DH, HID), jnp.float32) * s_q, 'Wk': jax.random.normal(ks[2], (KV * DH, HID), jnp.float32) * s_kv, 'Wv': jax.random.normal(ks[3], (KV * DH, HID), jnp.float32) * s_kv, 'Wo': jax.random.normal(ks[4], (HID, H * DH), jnp.float32) * s_o, 'q_norm_w': jnp.ones((DH,), jnp.float32), 'k_norm_w': jnp.ones((DH,), jnp.float32)}
    _L0_attn_in = _L0_attn_setup()

    def _L0_ffn_setup():
        import jax, jax.numpy as jnp
        import numpy as np
        GROUP = 16
        EPS = 1e-05

        def _dequant(q, scale):
            w = q.astype(jnp.float32) / 7.5 - 1.0
            return w * jnp.repeat(scale, GROUP, axis=1)

        def _qlora_linear(x, q, scale, bias, la, lb):
            w = _dequant(q, scale)
            base = jnp.einsum('btd,od->bto', x, w) + bias
            lora = jnp.einsum('btr,or->bto', jnp.einsum('btd,rd->btr', x, la), lb)
            return base + lora

        def _layernorm(x, g, b):
            mu = jnp.mean(x, axis=-1, keepdims=True)
            var = jnp.mean(jnp.square(x - mu), axis=-1, keepdims=True)
            return (x - mu) * jax.lax.rsqrt(var + EPS) * g + b
        key = jax.random.key(seed)
        ks = jax.random.split(key, 6)
        D, R, B, T = (128, 32, 8, 512)
        x = jax.random.normal(ks[0], (B, T, D), dtype=jnp.float32)
        qweights = jax.random.randint(ks[1], (6, D, D), 0, 16, dtype=jnp.int32)
        scales = jax.random.uniform(ks[2], (6, D, D // GROUP), dtype=jnp.float32)
        biases = jax.random.normal(ks[3], (6, D), dtype=jnp.float32) * 0.02
        lora_a = jax.random.normal(ks[4], (6, R, D), dtype=jnp.float32) * 0.02
        lora_b = jax.random.normal(ks[5], (6, D, R), dtype=jnp.float32) * 0.02
        ln_gamma = jnp.ones((3, D), dtype=jnp.float32)
        ln_beta = jnp.zeros((3, D), dtype=jnp.float32)
        return {'x': x, 'qweights': qweights, 'scales': scales, 'biases': biases, 'lora_a': lora_a, 'lora_b': lora_b, 'ln_gamma': ln_gamma, 'ln_beta': ln_beta}
    _L0_ffn_in = _L0_ffn_setup()
    _d = {'L0_attn_inputs': _L0_attn_in['inputs'], 'L0_attn_Wq': _L0_attn_in['Wq'], 'L0_attn_Wk': _L0_attn_in['Wk'], 'L0_attn_Wv': _L0_attn_in['Wv'], 'L0_attn_Wo': _L0_attn_in['Wo'], 'L0_attn_q_norm_w': _L0_attn_in['q_norm_w'], 'L0_attn_k_norm_w': _L0_attn_in['k_norm_w'], 'L0_ffn_qweights': _L0_ffn_in['qweights'], 'L0_ffn_scales': _L0_ffn_in['scales'], 'L0_ffn_biases': _L0_ffn_in['biases'], 'L0_ffn_lora_a': _L0_ffn_in['lora_a'], 'L0_ffn_lora_b': _L0_ffn_in['lora_b'], 'L0_ffn_ln_gamma': _L0_ffn_in['ln_gamma'], 'L0_ffn_ln_beta': _L0_ffn_in['ln_beta']}
    _x0 = _d['L0_attn_inputs']
    _d['L0_attn_inputs'] = jax.random.normal(jax.random.fold_in(jax.random.key(seed), 1), (4, 512, 128), dtype=_x0.dtype)
    del _x0
    return _d

def reference(L0_attn_inputs, L0_attn_Wq, L0_attn_Wk, L0_attn_Wv, L0_attn_Wo, L0_attn_q_norm_w, L0_attn_k_norm_w, L0_ffn_qweights, L0_ffn_scales, L0_ffn_biases, L0_ffn_lora_a, L0_ffn_lora_b, L0_ffn_ln_gamma, L0_ffn_ln_beta):

    def _L0_attn_ref(inputs, Wq, Wk, Wv, Wo, q_norm_w, k_norm_w):
        import jax, jax.numpy as jnp
        import numpy as np
        B, L, HID = (8, 1025, 128)
        H, KV, DH = (16, 4, 64)
        EPS = 1e-06
        ROPE_BASE = 10000.0

        def _rms_norm(x, w):
            var = jnp.mean(jnp.square(x), axis=-1, keepdims=True)
            return x * jax.lax.rsqrt(var + EPS) * w

        def _rotate_half(x):
            x1, x2 = jnp.split(x, 2, axis=-1)
            return jnp.concatenate([-x2, x1], axis=-1)

        def _rope_cache(seq_len, dim):
            inv_freq = 1.0 / ROPE_BASE ** (jnp.arange(0, dim, 2, dtype=jnp.float32) / dim)
            pos = jnp.arange(seq_len, dtype=jnp.float32)
            freqs = pos[:, None] * inv_freq[None, :]
            emb = jnp.concatenate([freqs, freqs], axis=-1)
            return (jnp.cos(emb), jnp.sin(emb))
        b, l, _ = inputs.shape
        q = (inputs @ Wq.T).reshape(b, l, H, DH)
        k = (inputs @ Wk.T).reshape(b, l, KV, DH)
        v = (inputs @ Wv.T).reshape(b, l, KV, DH)
        q = _rms_norm(q, q_norm_w).transpose(0, 2, 1, 3)
        k = _rms_norm(k, k_norm_w).transpose(0, 2, 1, 3)
        v = v.transpose(0, 2, 1, 3)
        l_img = l - 1
        cos, sin = _rope_cache(l_img, DH)
        cos = cos[None, None].astype(q.dtype)
        sin = sin[None, None].astype(q.dtype)
        q_img = q[:, :, 1:]
        k_img = k[:, :, 1:]
        q = jnp.concatenate([q[:, :, :1], q_img * cos + _rotate_half(q_img) * sin], axis=2)
        k = jnp.concatenate([k[:, :, :1], k_img * cos + _rotate_half(k_img) * sin], axis=2)
        rep = H // KV
        k = jnp.repeat(k, rep, axis=1)
        v = jnp.repeat(v, rep, axis=1)
        scores = jnp.einsum('bhqd,bhkd->bhqk', q, k)
        attn = jax.nn.softmax(scores.astype(jnp.float32), axis=-1).astype(q.dtype)
        out = jnp.einsum('bhqk,bhkd->bhqd', attn, v)
        out = out.transpose(0, 2, 1, 3).reshape(b, l, H * DH)
        return out @ Wo.T

    def _L0_ffn_ref(x, qweights, scales, biases, lora_a, lora_b, ln_gamma, ln_beta):
        import jax, jax.numpy as jnp
        import numpy as np
        GROUP = 16
        EPS = 1e-05

        def _dequant(q, scale):
            w = q.astype(jnp.float32) / 7.5 - 1.0
            return w * jnp.repeat(scale, GROUP, axis=1)

        def _qlora_linear(x, q, scale, bias, la, lb):
            w = _dequant(q, scale)
            base = jnp.einsum('btd,od->bto', x, w) + bias
            lora = jnp.einsum('btr,or->bto', jnp.einsum('btd,rd->btr', x, la), lb)
            return base + lora

        def _layernorm(x, g, b):
            mu = jnp.mean(x, axis=-1, keepdims=True)
            var = jnp.mean(jnp.square(x - mu), axis=-1, keepdims=True)
            return (x - mu) * jax.lax.rsqrt(var + EPS) * g + b
        h = x
        for blk in range(3):
            i0, i1 = (2 * blk, 2 * blk + 1)
            y = _qlora_linear(h, qweights[i0], scales[i0], biases[i0], lora_a[i0], lora_b[i0])
            y = _layernorm(y, ln_gamma[blk], ln_beta[blk])
            y = jax.nn.gelu(y, approximate=False)
            y = _qlora_linear(y, qweights[i1], scales[i1], biases[i1], lora_a[i1], lora_b[i1])
            h = y + h
        return h
    x = L0_attn_inputs
    xn = _layernorm(x, axis=-1)
    x = x + _L0_attn_ref(xn, L0_attn_Wq, L0_attn_Wk, L0_attn_Wv, L0_attn_Wo, L0_attn_q_norm_w, L0_attn_k_norm_w) + _L0_ffn_ref(xn, L0_ffn_qweights, L0_ffn_scales, L0_ffn_biases, L0_ffn_lora_a, L0_ffn_lora_b, L0_ffn_ln_gamma, L0_ffn_ln_beta)
    return x

_drawn_inputs = setup_inputs


def setup_inputs(seed=0):
    import zlib

    import numpy as np

    out = dict(_drawn_inputs(seed))
    spreads = {'L0_attn_q_norm_w': (1.0, 0.2),
     'L0_attn_k_norm_w': (1.0, 0.2),
     'L0_ffn_ln_gamma': (1.0, 0.2),
     'L0_ffn_ln_beta': (0.0, 0.1)}
    factors = {'L0_ffn_biases': 5.237, 'L0_ffn_lora_a': 5.305, 'L0_ffn_lora_b': 5.38}
    for name, (base, spread) in spreads.items():
        noise = np.random.default_rng([zlib.crc32(name.encode()), seed]).standard_normal(out[name].shape)
        drawn = base * np.exp(spread * noise) if base else spread * noise
        out[name] = jnp.asarray(drawn.astype(out[name].dtype))
    for name, factor in factors.items():
        out[name] = (out[name] * factor).astype(out[name].dtype)
    return out
```

```python
from contextlib import ExitStack

import numpy as np

import concourse.bass as bass
from concourse import mybir
from concourse.alu_op_type import AluOpType as ALU

F32 = mybir.dt.float32
F32R = mybir.dt.float32r
I32 = mybir.dt.int32
ACT = mybir.ActivationFunctionType
AX = mybir.AxisListType

B, L, D = 4, 512, 128
P = 128
NT = L // P
H, KV, DH = 16, 4, 64
HG = H // KV
NV = HG + 1
NQK = NV * DH
NPROJ = NQK + DH
RAW = NPROJ + 1
FB, R, QG = 3, 32, 16
LN_EPS, RMS_EPS = 1e-5, 1e-6
SLOTS = 16
GROUPS = 4

SCRATCH = {0: ("maxrow", 1), 1: ("ffn1", 0), 2: ("turn", 0), 3: ("turn", 1), 4: ("proj", 0), 5: ("proj", 1),
           6: ("proj", 2), 7: ("proj", 3), 8: ("ffn_turn", 0), 9: ("maxrow", 0), 10: ("turn", 2),
           11: ("out_turn", 0), 12: ("ffn2", 0), 13: ("out_turn", 1)}


def batch_uses(first, last):
    uses, count = {}, 0
    for g in range(GROUPS):
        for s in range(SLOTS):
            if s not in SCRATCH:
                continue
            kind, arg = SCRATCH[s]
            if g == 3 and kind in ("ffn1", "ffn_turn", "ffn2"):
                if kind != "ffn1" or first:
                    continue
                kind = "final"
            if kind == "turn" and last and g >= 2:
                continue
            if kind == "proj" and last and g >= 1:
                continue
            if kind == "out_turn" and first and g == 0:
                continue
            if kind == "maxrow" and arg == 0 and last and g == 3:
                continue
            uses[g, s] = (kind, arg, count)
            count += 1
    return uses, count


def wait(eng, sem, value):
    if not isinstance(value, int) or value > 0:
        eng.wait_ge(sem, value)


def attention_ffn(nc, x, wq, wk, wv, wo, q_w, k_w, qweights, scales, biases, biases_t, lora_a, lora_b_t,
                  gamma_t, beta_t, cos, sin, identity, out):
    with ExitStack() as ctx:
        def sb(name, shape, dt=F32):
            return ctx.enter_context(nc.sbuf_tensor(name, shape, dt))

        def sem(name):
            return ctx.enter_context(nc.semaphore(name))

        xn_t = sb("xn_t", [P, B * L])
        xn_cur = sb("xn_cur", [P, L])
        w_qkv = sb("w_qkv", [P, KV, NPROJ])
        w_o = sb("w_o", [P, H // 2, D])
        ident = sb("ident", [P, P])
        cos_w = sb("cos_w", [P, NT, NQK])
        sin_w = sb("sin_w", [P, NT, NQK])
        raw = [sb(f"raw{i}", [P, NT, RAW]) for i in range(GROUPS)]
        squares = sb("squares", [P, NT, NQK])
        crossed = sb("crossed", [P, NT, NQK])
        rotated = [sb(f"rotated{i}", [P, NT, NQK]) for i in range(2)]
        ss = sb("ss", [P, NT * NV])
        sum_eps = sb("sum_eps", [P, NT * NV])
        rms_rs = sb("rms_rs", [P, NT * NV])
        minus_half = sb("minus_half", [P, NT * NV])
        rms_eps = sb("rms_eps", [P, NT * NV])
        ln_eps = sb("ln_eps", [P, NT])
        q_split = [sb(f"q_split{i}", [P, HG, L], F32R) for i in range(GROUPS)]
        q_hi = [sb(f"q_hi{i}", [P, HG, L], F32R) for i in range(GROUPS)]
        k_hi = [sb(f"k_hi{i}", [P, L], F32R) for i in range(GROUPS)]
        k_lo = [sb(f"k_lo{i}", [P, L], F32R) for i in range(GROUPS)]
        neg_max = [sb(f"neg_max{i}", [P, HG * NT]) for i in range(GROUPS)]
        max_row = [sb(f"max_row{i}", [8, P], F32R) for i in range(2)]
        probs = [sb(f"probs{i}", [P, NT, L]) for i in range(2)]
        inv_sum = [sb(f"inv_sum{i}", [P, NT]) for i in range(2)]
        o_tok = [sb(f"o_tok{i}", [P, NT, HG * DH]) for i in range(2)]
        o_t = sb("o_t", [P, 2, L])
        ln_stats = sb("ln_stats", [P, B * NT, 6])
        ln_mv = sb("ln_mv", [P, B * NT, 2])
        ln_var = sb("ln_var", [P, B * NT])
        ln_rs = sb("ln_rs", [P, B * NT])
        w_ffn = sb("w_ffn", [P, 2 * FB, D])
        bias_row = sb("bias_row", [P, FB, D])
        bias_col = sb("bias_col", [P, 2 * FB])
        gam = sb("gam", [P, FB])
        bet = sb("bet", [P, FB])
        h = [sb(f"h{i}", [P, L]) for i in range(FB + 1)]
        y_tok = sb("y_tok", [P, NT, D])
        f_stats = sb("f_stats", [P, NT, 6])
        f_mv = sb("f_mv", [P, NT, 2])
        f_var = sb("f_var", [P, NT])
        f_rs = sb("f_rs", [P, NT])
        y_t = sb("y_t", [P, L])
        out_tok = sb("out_tok", [P, NT, D])

        def bank(name):
            return ctx.enter_context(nc.psum_tensor(name, [P, 512], F32))

        score_ps = [bank(f"score_ps{i}") for i in range(2)]
        max_ps = [bank(f"max_ps{i}") for i in range(2)]
        pv_ps = [bank(f"pv_ps{i}") for i in range(2)]
        scratch_ps = bank("scratch_ps")
        y_ps = bank("y_ps")

        x_in = [sem(f"x_in{b}") for b in range(B)]
        w_in = sem("w_in")
        tab_in = sem("tab_in")
        ffn_in = sem("ffn_in")
        x_again = sem("x_again")
        out_stored = sem("out_stored")
        consts_set = sem("consts_set")
        tables_set = sem("tables_set")
        ln_stat = sem("ln_stat")
        ln_agg = sem("ln_agg")
        ln_varred = sem("ln_varred")
        ln_rsdone = sem("ln_rsdone")
        xn_tok_ready = sem("xn_tok_ready")
        xn_cur_ready = sem("xn_cur_ready")
        deq = sem("deq")
        lora_ready = sem("lora_ready")
        h0_ready = sem("h0_ready")
        w_ffn_ready = sem("w_ffn_ready")
        scratch_full = sem("scratch_full")
        scratch_free = sem("scratch_free")
        squared = sem("squared")
        ss_ready = sem("ss_ready")
        pool_step = sem("pool_step")
        rotated_ready = sem("rotated_ready")
        hi_ready = sem("hi_ready")
        hi_copied = [sem(f"hi_copied{i}") for i in range(2)]
        max_full = sem("max_full")
        max_done = sem("max_done")
        max_placed = sem("max_placed")
        score_full = sem("score_full")
        exp_done = sem("exp_done")
        pv_full = sem("pv_full")
        inv_ready = sem("inv_ready")
        o_ready = sem("o_ready")
        y_full = sem("y_full")
        y_t_ready = sem("y_t_ready")
        f_stat = sem("f_stat")
        f_agg = sem("f_agg")
        f_varred = sem("f_varred")
        f_rsdone = sem("f_rsdone")
        f_norm = sem("f_norm")

        x_tok = probs[0][:].rearrange("p a b -> p (a b)").rearrange("p (t d) -> p t d", d=D)
        xn_tok = x_tok
        spare = probs[1][:].rearrange("p a b -> p (a b)")
        q_int = spare[:, 0:768].bitcast(I32)
        cos_sb = spare[:, 768:1024].rearrange("p (t d) -> p t d", d=DH)
        sin_sb = spare[:, 1024:1280].rearrange("p (t d) -> p t d", d=DH)
        w_rep = spare[:, 1280:1600].rearrange("p (j d) -> p j d", d=DH)
        w_swap = spare[:, 1600:1920].rearrange("p (j d) -> p j d", d=DH)
        la = rotated[0][:].rearrange("p a b -> p (a b)")[0:R, 0:768].rearrange("r (i d) -> r i d", d=D)
        lb = rotated[1][:].rearrange("p a b -> p (a b)")[0:R, 0:768].rearrange("r (i d) -> r i d", d=D)
        act_t = y_tok[:].rearrange("p t d -> p (t d)")
        deq_w = squares[:].rearrange("p a b -> p (a b)")[:, 0:2 * FB * D]
        scale_rep = crossed[:].rearrange("p a b -> p (a b)")[:, 0:2 * FB * D]

        PRO = [("xn_turn", 0)] + [("proj", m, t) for m in range(2) for t in range(NT)]
        PRO += [("xn_turn", b) for b in range(1, B)]
        PRO += [("turn", 0, j) for j in range(3)] + [("proj", 2, t) for t in range(NT)]
        PRO += [("maxrow", 0)] + [("turn", 1, j) for j in range(3)]
        pro = {use: n for n, use in enumerate(PRO)}
        kinds = {"first": batch_uses(True, False), "mid": batch_uses(False, False), "last": batch_uses(False, True)}

        def uses_before(kind, b):
            if kind == "first":
                return len(PRO)
            n = len(PRO) + kinds["first"][1]
            if kind == "mid":
                return (b - 1) * kinds["mid"][1] + n
            return n + (B - 2) * kinds["mid"][1]

        EPI = uses_before("last", B - 1) + kinds["last"][1]

        def use_at(kind, b, g, s):
            use = kinds[kind][0].get((g, s))
            return use and (use[0], use[1], uses_before(kind, b) + use[2])

        def batches(eng, body):
            body("first", 0)
            with eng.Fori(1, B - 1) as b:
                body("mid", b)
            body("last", B - 1)

        half = DH // 2
        block = ctx.enter_context(nc.Block())

        @block.sync
        def _(sp):
            def load(dst, src, s):
                sp.dma_start(dst, src).then_inc(s, 16)

            for b in range(B):
                load(x_tok[:, b * NT:(b + 1) * NT, :], x[b].rearrange("(t p) d -> p t d", p=P), x_in[b])
                if b == 0:
                    load(ident[:], identity, w_in)
                    load(w_qkv[:, :, 0:HG * DH], wq.rearrange("d (g n) -> d g n", g=KV), w_in)
                    load(w_qkv[:, :, HG * DH:NQK], wk.rearrange("d (g n) -> d g n", g=KV), w_in)
                    load(w_qkv[:, :, NQK:NPROJ], wv.rearrange("d (g n) -> d g n", g=KV), w_in)
            load(w_o[:], wo.rearrange("(c p) n -> p c n", p=P), w_in)

            def place_max(u, slot, part):
                sp.wait_ge(scratch_free, u + 1)
                sp.dma_start(q_hi[slot][64:65, 2 * part:2 * part + 2, :].bitcast(F32),
                             max_row[part][:].bitcast(F32)).then_inc(max_placed, 16)

            def copy_hi(m, slot, pair):
                sp.wait_ge(hi_ready, m * 6 + 4 + 2 * pair)
                sp.dma_start(q_split[slot][0:64, 2 * pair:2 * pair + 2, :].bitcast(F32),
                             q_hi[slot][0:64, 2 * pair:2 * pair + 2, :].bitcast(F32)).then_inc(hi_copied[pair], 16)

            def body(kind, b):
                for g in range(GROUPS):
                    n = b * GROUPS + g
                    place_max(use_at(kind, b, g, 0)[2], g, 1)
                    if use_at(kind, b, g, 3):
                        copy_hi(n + 2, (g + 2) % GROUPS, 0)
                    if not (kind == "last" and g == 3):
                        place_max(use_at(kind, b, g, 9)[2], (g + 1) % GROUPS, 0)
                    if use_at(kind, b, g, 10):
                        copy_hi(n + 2, (g + 2) % GROUPS, 1)
                    if g == 0 and kind != "first":
                        wait(sp, out_stored, 16 * (b - 1))
                        src = x[B - 2:B - 1] if kind == "last" else x[bass.ds(b - 1, 1)]
                        sp.dma_start(out_tok[:], src.rearrange("o (t p) d -> p (o t) d", p=P)).then_inc(x_again, 16)
                    if g == 3 and kind != "first":
                        sp.wait_ge(scratch_free, use_at(kind, b, 3, 1)[2] + 1)
                        dst = out[B - 2:B - 1] if kind == "last" else out[bass.ds(b - 1, 1)]
                        sp.dma_start(dst.rearrange("o (t p) d -> p (o t) d", p=P), out_tok[:]).then_inc(out_stored, 16)

            copy_hi(0, 0, 0)
            copy_hi(0, 0, 1)
            place_max(pro["maxrow", 0], 0, 0)
            copy_hi(1, 1, 0)
            copy_hi(1, 1, 1)
            batches(sp, body)
            sp.wait_ge(out_stored, 16 * (B - 1))
            sp.dma_start(out_tok[:], x[B - 1].rearrange("(t p) d -> p t d", p=P)).then_inc(x_again, 16)
            sp.wait_ge(scratch_free, EPI + 3)
            sp.dma_start(out[B - 1].rearrange("(t p) d -> p t d", p=P), out_tok[:]).then_inc(out_stored, 16)
            sp.wait_ge(out_stored, 16 * B)

        @block.gpsimd
        def _(pool):
            def load(dst, src, s):
                pool.dma_start(dst, src).then_inc(s, 16)

            load(cos_sb, cos.rearrange("(t p) d -> p t d", p=P), tab_in)
            load(sin_sb, sin.rearrange("(t p) d -> p t d", p=P), tab_in)
            for j, w in [(j, q_w if j < HG else k_w) for j in range(NV)]:
                load(w_rep[:, j, :], w.partition_broadcast(P), tab_in)
                load(w_swap[:, j, 0:half], w[half:DH].partition_broadcast(P), tab_in)
                load(w_swap[:, j, half:DH], w[0:half].partition_broadcast(P), tab_in)
            for i in range(GROUPS):
                nc.gpsimd.memset(raw[i][:, :, NPROJ:RAW], 1.0)
            nc.gpsimd.memset(rms_eps[:], DH * RMS_EPS)
            nc.gpsimd.memset(ln_eps[:], LN_EPS)
            nc.gpsimd.memset(minus_half[:], -0.5).then_inc(consts_set, 1)
            pool.wait_ge(consts_set, 1)

            for b in range(B):
                tiles = slice(b * NT, (b + 1) * NT)
                pool.wait_ge(ln_agg, b + 1)
                nc.gpsimd.tensor_tensor(ln_var[:, tiles], ln_mv[:, tiles, 1], ln_eps[:], ALU.add).then_inc(ln_varred, 1)
                pool.wait_ge(ln_varred, b + 1)
                nc.gpsimd.tensor_tensor(ln_rs[:, tiles], ln_var[:, tiles], minus_half[:, 0:NT],
                                        ALU.pow).then_inc(ln_rsdone, 1)
            pool.wait_ge(tab_in, 16 * (2 + 3 * NV))
            for t in range(NT):
                for dst, tab, w in ((cos_w, cos_sb, w_rep), (sin_w, sin_sb, w_swap)):
                    nc.gpsimd.tensor_tensor(dst[:, t, :].rearrange("p (j d) -> p j d", d=DH), w,
                                            tab[:, t, :].unsqueeze(1).to_broadcast([P, NV, DH]),
                                            ALU.mult).then_inc(tables_set, 1)

            def rotate(m, u, slot, parity):
                r, dst = raw[slot], rotated[parity]
                pool.wait_ge(scratch_free, u + 1)
                nc.gpsimd.tensor_tensor(squares[:], r[:, :, 0:NQK], r[:, :, 0:NQK], ALU.mult).then_inc(squared, 1)
                nc.gpsimd.tensor_tensor(dst[:], r[:, :, 0:NQK], cos_w[:], ALU.mult).then_inc(pool_step, 1)
                for s in range(2):
                    for_half = "p t (j s d) -> p t j s d"
                    nc.gpsimd.tensor_tensor(
                        crossed[:].rearrange(for_half, s=2, d=half)[:, :, :, s, :],
                        r[:, :, 0:NQK].rearrange(for_half, s=2, d=half)[:, :, :, 1 - s, :],
                        sin_w[:].rearrange(for_half, s=2, d=half)[:, :, :, s, :], ALU.mult).then_inc(pool_step, 1)
                pool.wait_ge(ss_ready, m + 1)
                nc.gpsimd.tensor_tensor(sum_eps[:], ss[:], rms_eps[:], ALU.add).then_inc(pool_step, 1)
                pool.wait_ge(pool_step, m * 6 + 4)
                nc.gpsimd.tensor_tensor(rms_rs[:], sum_eps[:], minus_half[:], ALU.pow).then_inc(pool_step, 1)
                nc.gpsimd.tensor_tensor(dst[:], dst[:], crossed[:], ALU.add).then_inc(pool_step, 1)
                pool.wait_ge(pool_step, m * 6 + 6)
                d3 = dst[:].rearrange("p t (j d) -> p (t j) d", d=DH)
                nc.gpsimd.tensor_tensor(d3, d3, rms_rs[:].unsqueeze(2).to_broadcast([P, NT * NV, DH]),
                                        ALU.mult).then_inc(rotated_ready, 1)

            pool.wait_ge(tables_set, 2 * NT)
            pool.wait_ge(w_ffn_ready, 1)
            for m in range(3):
                rotate(m, pro["proj", m, NT - 1], m, m % 2)

            def body(kind, b):
                for g in range(GROUPS):
                    n = b * GROUPS + g
                    if g < FB:
                        k = b * FB + g
                        pool.wait_ge(f_agg, k + 1)
                        nc.gpsimd.tensor_tensor(f_var[:], f_mv[:, :, 1], ln_eps[:], ALU.add).then_inc(f_varred, 1)
                        pool.wait_ge(f_varred, k + 1)
                        nc.gpsimd.tensor_tensor(f_rs[:], f_var[:], minus_half[:, 0:NT], ALU.pow).then_inc(f_rsdone, 1)
                    if use_at(kind, b, g, 7):
                        rotate(n + 3, use_at(kind, b, g, 7)[2], (g + 3) % GROUPS, (g + 3) % 2)

            batches(pool, body)

        @block.scalar
        def _(act):
            def load(dst, src, s):
                act.dma_start(dst, src).then_inc(s, 16)

            load(q_int.rearrange("p (i o) -> p i o", o=D), qweights.rearrange("i d o -> d i o"), ffn_in)
            for q in range(D // QG):
                load(scale_rep[q * QG:(q + 1) * QG, :].rearrange("p (i o) -> p i o", o=D),
                     scales[:, q, :].partition_broadcast(QG), ffn_in)
            load(la, lora_a.rearrange("i r d -> r i d"), ffn_in)
            load(lb, lora_b_t.rearrange("i r o -> r i o"), ffn_in)
            for i in range(FB):
                load(bias_row[:, i, :], biases[2 * i].partition_broadcast(P), ffn_in)
            load(bias_col[:], biases_t, ffn_in)
            load(gam[:], gamma_t, ffn_in)
            load(bet[:], beta_t, ffn_in)

            def copy(u, dst, src):
                act.wait_ge(scratch_full, u + 1)
                nc.scalar.activation(dst, src, ACT.Copy).then_inc(scratch_free, 1)

            def copy_raw(u, slot, t):
                copy(u, raw[slot][:, t, 0:NPROJ], scratch_ps[:, 0:NPROJ])

            def round_hi(u, slot, j):
                act.wait_ge(scratch_full, u + 1)
                for k in range(2):
                    if j == 0:
                        dst, src = k_hi[slot][64 * k:64 * k + 64, :], scratch_ps[64:128, :]
                    else:
                        dst, src = q_hi[slot][0:64, 2 * j - 2 + k, :], scratch_ps[64 * k:64 * k + 64, :]
                    nc.scalar.activation(dst, src, ACT.Copy).then_inc(hi_ready, 1)

            def copy_max(u, part, placed):
                wait(act, max_placed, placed)
                copy(u, max_row[part][:], scratch_ps[0:8, 0:P])

            def exp(n, s):
                j = n * SLOTS + s
                if s % NT == 0:
                    wait(act, pv_full, n * HG + s // NT - 1)
                act.wait_ge(score_full, j + 1)
                nc.scalar.activation(probs[s // NT % 2][:, s % NT, :], score_ps[s % 2][:],
                                     ACT.Exp).then_inc(exp_done, 1)

            for use in PRO:
                u = pro[use]
                if use[0] == "xn_turn":
                    copy(u, xn_t[:, use[1] * L:(use[1] + 1) * L], scratch_ps[:])
                elif use[0] == "proj":
                    copy_raw(u, use[1], use[2])
                elif use[0] == "turn":
                    round_hi(u, use[1], use[2])
                else:
                    copy_max(u, 0, 0)

            def body(kind, b):
                for g in range(GROUPS):
                    n = b * GROUPS + g
                    for s in range(SLOTS):
                        exp(n, s)
                        use = use_at(kind, b, g, s)
                        if not use:
                            continue
                        what, arg, u = use
                        if what == "proj":
                            copy_raw(u, (g + 3) % GROUPS, arg)
                        elif what == "turn":
                            round_hi(u, (g + 2) % GROUPS, arg)
                        elif what == "maxrow":
                            copy_max(u, arg, n * 32 + (0 if arg else 16))
                        elif what == "out_turn":
                            copy(u, o_t[:, arg, :], scratch_ps[:])
                        elif what == "ffn_turn":
                            act.wait_ge(scratch_full, u + 1)
                            nc.scalar.activation(act_t, scratch_ps[:], ACT.Gelu, bias=bet[:, g:g + 1],
                                                 scale=gam[:, g:g + 1]).then_inc(scratch_free, 1)

            batches(act, body)
            copy(EPI, o_t[:, 0, :], scratch_ps[:])
            copy(EPI + 1, o_t[:, 1, :], scratch_ps[:])

        @block.tensor
        def _(pe):
            def begin(u):
                wait(pe, scratch_free, u)

            def turn4(u, tiles):
                begin(u)
                for c in range(NT):
                    last = nc.tensor.transpose(scratch_ps[:, c * P:(c + 1) * P], tiles(c), ident[:])
                last.then_inc(scratch_full, 1)

            def project(u, g, t):
                begin(u)
                nc.tensor.matmul(scratch_ps[:, 0:NPROJ], xn_cur[:, t * P:(t + 1) * P], w_qkv[:, g, :],
                                 start=True, stop=True).then_inc(scratch_full, 1)

            def turn_heads(u, m, parity, j):
                pe.wait_ge(rotated_ready, m + 1)
                begin(u)
                lo = NQK - P if j == 0 else (j - 1) * P
                for t in range(NT):
                    last = nc.tensor.transpose(scratch_ps[:, t * P:(t + 1) * P],
                                               rotated[parity][:, t, lo:lo + P], ident[:])
                last.then_inc(scratch_full, 1)

            def max_tile(m, slot, s):
                if s % 8 == 0:
                    pe.wait_ge(hi_copied[s // 8], m * 16 + 16)
                wait(pe, max_done, m * SLOTS + s - 1)
                nc.tensor.matmul(max_ps[s % 2][:], q_split[slot][:, s // NT, (s % NT) * P:(s % NT + 1) * P],
                                 k_hi[slot][:], start=True, stop=True).then_inc(max_full, 1)

            def max_row_turn(u, m, slot, part):
                pe.wait_ge(max_done, m * SLOTS + 8 * part + 8)
                begin(u)
                nc.tensor.transpose(scratch_ps[0:8, 0:P], neg_max[slot][:, 8 * part:8 * part + 8],
                                    ident[:]).then_inc(scratch_full, 1)

            def score_tile(n, g, s):
                hd, c = s // NT, s % NT
                if c == 0 and hd % 2 == 0:
                    pe.wait_ge(max_placed, n * 32 + 16 + 8 * hd)
                wait(pe, exp_done, n * SLOTS + s - 1)
                keys = slice(c * P, (c + 1) * P)
                nc.tensor.matmul(score_ps[s % 2][:], k_hi[g][:, keys], q_split[g][:, hd, :], start=True, stop=False)
                nc.tensor.matmul(score_ps[s % 2][:], k_lo[g][0:65, keys], q_hi[g][0:65, hd, :], start=False,
                                 stop=True).then_inc(score_full, 1)

            def pv_tile(head, slot, hd, c):
                if c == 0:
                    pe.wait_ge(exp_done, head * NT + NT)
                    wait(pe, o_ready, head - 1)
                for kc in range(NT):
                    last = nc.tensor.matmul(pv_ps[hd % 2][:, c * 65:(c + 1) * 65],
                                            probs[hd % 2][:, kc, c * P:(c + 1) * P],
                                            raw[slot][:, kc, NQK:RAW], start=(kc == 0), stop=(kc == NT - 1))
                if c == NT - 1:
                    last.then_inc(pv_full, 1)

            def out_turn(u, heads, parity, pair):
                pe.wait_ge(o_ready, heads)
                turn4(u, lambda t: o_tok[parity][:, t, pair * P:(pair + 1) * P])

            def out_project(u, b, g, pair):
                pe.wait_ge(scratch_free, u + 1)
                first, last = (g == 0 and pair == 0), (g == 3 and pair == 1)
                if first:
                    wait(pe, y_t_ready, b)
                mm = nc.tensor.matmul(y_ps[:], w_o[:, 2 * g + pair, :], o_t[:, pair, :], start=first, stop=last)
                if last:
                    mm.then_inc(y_full, 1)

            pe.wait_ge(w_in, 16 * 5)
            for use in PRO:
                u = pro[use]
                if use[0] == "xn_turn":
                    if use[1] == 1:
                        pe.wait_ge(ffn_in, 16 * (3 + D // QG + FB + 3))
                        for i in range(2 * FB):
                            mm = nc.tensor.matmul(pv_ps[i // 4][:, i % 4 * D:(i % 4 + 1) * D], la[:, i, :],
                                                  lb[:, i, :], start=True, stop=True)
                        mm.then_inc(lora_ready, 1)
                    pe.wait_ge(xn_tok_ready, use[1] + 1)
                    turn4(u, lambda t: xn_tok[:, use[1] * NT + t, :])
                elif use[0] == "proj":
                    pe.wait_ge(xn_cur_ready, 1)
                    project(u, use[1], use[2])
                elif use[0] == "maxrow":
                    begin(u)
                    for s in range(8):
                        max_tile(0, 0, s)
                    max_row_turn(u, 0, 0, 0)
                else:
                    turn_heads(u, use[1], use[1] % 2, use[2])
                    if use[1] == 1:
                        max_tile(0, 0, 8 + use[2])
            for s in range(8 + 3, SLOTS):
                max_tile(0, 0, s)

            def body(kind, b):
                for g in range(GROUPS):
                    n = b * GROUPS + g
                    for s in range(SLOTS):
                        score_tile(n, g, s)
                        use = use_at(kind, b, g, s)
                        what, arg, u = use or (None, None, None)
                        if what == "proj":
                            pe.wait_ge(xn_cur_ready, b + (1 if g == 0 else 2))
                            project(u, (g + 3) % GROUPS, arg)
                        elif what == "turn":
                            turn_heads(u, n + 2, g % 2, arg)
                        elif what == "maxrow" and arg == 1:
                            max_row_turn(u, n, g, 1)
                        elif what == "maxrow":
                            max_row_turn(u, n + 1, (g + 1) % GROUPS, 0)
                        elif what == "out_turn":
                            out_turn(u, n * HG, (g + 1) % 2, arg)
                        elif what == "ffn1":
                            if g == 0:
                                pe.wait_ge(h0_ready, b + 1)
                            begin(u)
                            for t in range(NT):
                                mm = nc.tensor.matmul(scratch_ps[:, t * P:(t + 1) * P], h[g][:, t * P:(t + 1) * P],
                                                      w_ffn[:, 2 * g, :], start=True, stop=True)
                            mm.then_inc(scratch_full, 1)
                        elif what == "ffn_turn":
                            pe.wait_ge(f_norm, b * FB + g + 1)
                            turn4(u, lambda t: y_tok[:, t, :])
                        elif what == "ffn2":
                            begin(u)
                            nc.tensor.matmul(scratch_ps[:], w_ffn[:, 2 * g + 1, :], act_t, start=True,
                                             stop=True).then_inc(scratch_full, 1)
                        elif what == "final":
                            pe.wait_ge(y_t_ready, b)
                            turn4(u, lambda t: y_t[:, t * P:(t + 1) * P])
                        if s in (12, 14) and not (kind == "first" and g == 0):
                            pair = s // 2 - 6
                            out_project(use_at(kind, b, g, 11 + 2 * pair)[2], b, (g + 3) % GROUPS, pair)
                        if not (kind == "last" and g == 3):
                            max_tile(n + 1, (g + 1) % GROUPS, s)
                        hd = s // NT - 1
                        if hd >= 0:
                            pv_tile(n * HG + hd, g, hd, s % NT)
                        elif not (kind == "first" and g == 0):
                            pv_tile(n * HG - 1, (g + 3) % GROUPS, HG - 1, s % NT)

            batches(pe, body)

            for c in range(NT):
                pv_tile(B * H - 1, 3, HG - 1, c)
            for pair in range(2):
                out_turn(EPI + pair, B * H, 1, pair)
            for pair in range(2):
                out_project(EPI + pair, B - 1, 3, pair)
            pe.wait_ge(y_t_ready, B)
            turn4(EPI + 2, lambda t: y_t[:, t * P:(t + 1) * P])

        @block.vector
        def _(dve):
            def layernorm_x(b):
                tiles = range(b * NT, (b + 1) * NT)
                dve.wait_ge(x_in[b], 16)
                for t in tiles:
                    last = nc.vector.bn_stats(ln_stats[:, t, :], x_tok[:, t, :])
                last.then_inc(ln_stat, 1)
                dve.wait_ge(ln_stat, b + 1)
                for t in tiles:
                    last = nc.vector.bn_aggr(ln_mv[:, t, :], ln_stats[:, t, :])
                last.then_inc(ln_agg, 1)
                dve.wait_ge(ln_rsdone, b + 1)
                for t in tiles:
                    last = nc.vector.tensor_scalar(xn_tok[:, t, :], x_tok[:, t, :], ln_mv[:, t, 0:1],
                                                   ln_rs[:, t:t + 1], ALU.subtract, ALU.mult)
                last.then_inc(xn_tok_ready, 1)

            def sum_squares(m):
                dve.wait_ge(squared, m + 1)
                nc.vector.tensor_reduce(ss[:], squares[:].rearrange("p t (j d) -> p (t j) d", d=DH), AX.X,
                                        ALU.add).then_inc(ss_ready, 1)

            def split(u, m, slot, j):
                dve.wait_ge(scratch_full, u + 1)
                dve.wait_ge(hi_ready, m * 6 + 2 * j + 2)
                if j == 0:
                    last = nc.vector.tensor_tensor(k_lo[slot][0:64, :], scratch_ps[64:128, :],
                                                   k_hi[slot][0:64, :].bitcast(F32), ALU.subtract)
                else:
                    for k in range(2):
                        head = 2 * j - 2 + k
                        last = nc.vector.tensor_tensor(q_split[slot][64:128, head, :], scratch_ps[64 * k:64 * k + 64, :],
                                                       q_hi[slot][0:64, head, :].bitcast(F32), ALU.subtract)
                last.then_inc(scratch_free, 1)

            def reduce_max(m, slot, s):
                dve.wait_ge(max_full, m * SLOTS + s + 1)
                nc.vector.tensor_reduce(neg_max[slot][:, s:s + 1], max_ps[s % 2][:], AX.X, ALU.max,
                                        negate=True).then_inc(max_done, 1)

            def normalise(head, hd, parity):
                dve.wait_ge(pv_full, head + 1)
                pv = pv_ps[hd % 2][:, 0:NT * 65].rearrange("p (c d) -> p c d", d=65)
                nc.vector.reciprocal(inv_sum[hd % 2][:], pv[:, :, DH]).then_inc(inv_ready, 1)
                dve.wait_ge(inv_ready, head + 1)
                nc.vector.tensor_tensor(o_tok[parity][:, :, hd * DH:(hd + 1) * DH], pv[:, :, 0:DH],
                                        inv_sum[hd % 2][:].unsqueeze(2).to_broadcast([P, NT, DH]),
                                        ALU.mult).then_inc(o_ready, 1)

            def add_streams(b):
                dve.wait_ge(y_full, b)
                nc.vector.tensor_tensor(y_t[:], y_ps[:], h[FB][:], ALU.add).then_inc(y_t_ready, 1)

            def final_rows(u, b):
                dve.wait_ge(x_again, b * 16)
                dve.wait_ge(scratch_full, u + 1)
                rows = out_tok[:].rearrange("p t d -> p (t d)")
                nc.vector.tensor_tensor(rows, scratch_ps[:], rows, ALU.add).then_inc(scratch_free, 1)

            for i in range(GROUPS):
                nc.vector.memset(k_lo[i][64:65, :].bitcast(F32), 1.0)
            layernorm_x(0)
            dve.wait_ge(scratch_free, pro["xn_turn", 0] + 1)
            nc.vector.tensor_copy(xn_cur[:], xn_t[:, 0:L]).then_inc(xn_cur_ready, 1)
            for b in range(1, B):
                layernorm_x(b)
            dve.wait_ge(ffn_in, 16 * (3 + D // QG + FB + 3))
            nc.vector.tensor_scalar(deq_w, q_int, 1.0 / 7.5, -1.0, ALU.mult, ALU.add).then_inc(deq, 1)
            dve.wait_ge(deq, 1)
            nc.vector.tensor_tensor(deq_w, deq_w, scale_rep, ALU.mult).then_inc(deq, 1)
            dve.wait_ge(deq, 2)
            dve.wait_ge(lora_ready, 1)
            w_flat = w_ffn[:].rearrange("p i o -> p (i o)")
            nc.vector.tensor_tensor(w_flat[:, 0:4 * D], deq_w[:, 0:4 * D], pv_ps[0][:], ALU.add)
            nc.vector.tensor_tensor(w_flat[:, 4 * D:6 * D], deq_w[:, 4 * D:6 * D], pv_ps[1][:, 0:2 * D],
                                    ALU.add).then_inc(w_ffn_ready, 1)
            sum_squares(0)
            sum_squares(1)
            for use in PRO:
                if use[0] == "turn":
                    split(pro[use], use[1], use[1], use[2])
                    if use[1] == 1:
                        reduce_max(0, 0, 8 + use[2])
                elif use[0] == "maxrow":
                    sum_squares(2)
                    for s in range(8):
                        reduce_max(0, 0, s)
            for s in range(8 + 3, SLOTS):
                reduce_max(0, 0, s)

            def body(kind, b):
                for g in range(GROUPS):
                    n = b * GROUPS + g
                    for s in range(SLOTS):
                        if s % NT == 0 and not (kind == "first" and g == 0 and s < 8):
                            hd = s // NT - 2
                            normalise(n * HG + hd, hd % HG, g % 2 if hd >= 0 else (g + 1) % 2)
                        if g == 0 and s == 0:
                            nc.vector.tensor_copy(h[0][:], xn_t[:, bass.ds(b * L, L)] if kind == "mid" else
                                                  xn_t[:, b * L:(b + 1) * L]).then_inc(h0_ready, 1)
                        if g == 1 and s == 0 and kind != "last":
                            nc.vector.tensor_copy(xn_cur[:], xn_t[:, bass.ds((b + 1) * L, L)] if kind == "mid" else
                                                  xn_t[:, L:2 * L]).then_inc(xn_cur_ready, 1)
                        if g < FB and s == 4:
                            dve.wait_ge(f_rsdone, b * FB + g + 1)
                            for t in range(NT):
                                last = nc.vector.tensor_scalar(y_tok[:, t, :], y_tok[:, t, :], f_mv[:, t, 0:1],
                                                               f_rs[:, t:t + 1], ALU.subtract, ALU.mult)
                            last.then_inc(f_norm, 1)
                        if s == 12 and use_at(kind, b, g, 7):
                            sum_squares(n + 3)
                        what, arg, u = use_at(kind, b, g, s) or (None, None, None)
                        if what == "turn":
                            split(u, n + 2, (g + 2) % GROUPS, arg)
                        elif what == "ffn1":
                            k = b * FB + g + 1
                            dve.wait_ge(scratch_full, u + 1)
                            nc.vector.tensor_tensor(y_tok[:], scratch_ps[:].rearrange("p (t d) -> p t d", d=D),
                                                    bias_row[:, g, :].unsqueeze(1).to_broadcast([P, NT, D]),
                                                    ALU.add).then_inc(scratch_free, 1)
                            dve.wait_ge(scratch_free, u + 1)
                            for t in range(NT):
                                last = nc.vector.bn_stats(f_stats[:, t, :], y_tok[:, t, :])
                            last.then_inc(f_stat, 1)
                        elif what == "ffn2":
                            dve.wait_ge(scratch_full, u + 1)
                            nc.vector.scalar_tensor_tensor(
                                out=h[g + 1][:], in0=scratch_ps[:], scalar=bias_col[:, 2 * g + 1:2 * g + 2],
                                in1=h[g][:], op0=ALU.add, op1=ALU.add).then_inc(scratch_free, 1)
                        elif what == "final":
                            final_rows(u, b)
                        if s == 15 and g == 0 and kind != "first":
                            add_streams(b)
                        if what == "ffn1":
                            dve.wait_ge(f_stat, k)
                        if not (kind == "last" and g == 3):
                            reduce_max(n + 1, (g + 1) % GROUPS, s)
                        if what == "ffn1":
                            for t in range(NT):
                                last = nc.vector.bn_aggr(f_mv[:, t, :], f_stats[:, t, :])
                            last.then_inc(f_agg, 1)

            batches(dve, body)
            for head in (B * H - 2, B * H - 1):
                normalise(head, head % HG, 1)
            add_streams(B)
            final_rows(EPI + 2, B)


def kernel(**inputs):
    import concourse.bacc as bacc
    from concourse.bass_utils import run_bass_kernel_spmd

    given = {name.replace("L0_", ""): np.asarray(a) for name, a in inputs.items()}
    t = np.ascontiguousarray

    inv_freq = (1.0 / 10000.0 ** (np.arange(0, DH, 2, dtype=np.float32) / DH)).astype(np.float32)
    freqs = np.arange(L - 1, dtype=np.float32)[:, None] * inv_freq[None, :]
    cos, sin = np.ones((L, DH), np.float32), np.zeros((L, DH), np.float32)
    cos[1:] = np.cos(np.concatenate([freqs, freqs], 1))
    sin[1:] = np.concatenate([-np.sin(freqs), np.sin(freqs)], 1)

    arrays = {
        "x": t(given["attn_inputs"]),
        "wq": t(given["attn_Wq"].T), "wk": t(given["attn_Wk"].T), "wv": t(given["attn_Wv"].T),
        "wo": t(given["attn_Wo"].T),
        "q_w": t(given["attn_q_norm_w"]), "k_w": t(given["attn_k_norm_w"]),
        "qweights": t(given["ffn_qweights"].transpose(0, 2, 1)), "scales": t(given["ffn_scales"].transpose(0, 2, 1)),
        "biases": t(given["ffn_biases"]), "biases_t": t(given["ffn_biases"].T),
        "lora_a": t(given["ffn_lora_a"]), "lora_b_t": t(given["ffn_lora_b"].transpose(0, 2, 1)),
        "gamma_t": t(given["ffn_ln_gamma"].T), "beta_t": t(given["ffn_ln_beta"].T),
        "cos": cos * np.float32(DH ** 0.5), "sin": sin * np.float32(DH ** 0.5), "identity": np.eye(P, dtype=np.float32),
    }
    nc = bacc.Bacc("TRN2", target_bir_lowering=False, num_devices=1)
    aps = {name: nc.dram_tensor(name, a.shape, mybir.dt.from_np(a.dtype), kind="ExternalInput").ap()
           for name, a in arrays.items()}
    out = nc.dram_tensor("out", (B, L, D), F32, kind="ExternalOutput").ap()
    attention_ffn(nc, out=out, **aps)
    result = run_bass_kernel_spmd(nc, [arrays], core_ids=[0])
    return result.results[0]["out"]
```

```python
from contextlib import ExitStack

import numpy as np

import concourse.bass as bass
from concourse import mybir
from concourse.alu_op_type import AluOpType as ALU

F32 = mybir.dt.float32
F32R = mybir.dt.float32r
I32 = mybir.dt.int32
ACT = mybir.ActivationFunctionType
AX = mybir.AxisListType

B, L, D = 4, 512, 128
P = 128
NT = L // P
H, KV, DH = 16, 4, 64
HG = H // KV
NV = HG + 1
NQK = NV * DH
NPROJ = NQK + DH
RAW = NPROJ + 1
FB, R, QG = 3, 32, 16
LN_EPS, RMS_EPS = 1e-5, 1e-6
SLOTS = 16
GROUPS = 4

SCRATCH = {0: ("maxrow", 1), 1: ("ffn1", 0), 2: ("turn", 0), 3: ("turn", 1), 4: ("proj", 0), 5: ("proj", 1),
           6: ("proj", 2), 7: ("proj", 3), 8: ("ffn_turn", 0), 9: ("maxrow", 0), 10: ("turn", 2),
           11: ("out_turn", 0), 12: ("out_turn", 1), 13: ("out", 0), 14: ("ffn2", 0), 15: ("final", 0)}


def batch_uses(first, last):
    uses, count = {}, 0
    for g in range(GROUPS):
        for s in range(SLOTS):
            kind, arg = SCRATCH[s]
            absent = {
                "ffn1": g == FB, "ffn_turn": g == FB, "ffn2": g == FB,
                "turn": last and g >= 2, "proj": last and g >= 1,
                "out_turn": first and g == 0, "out": first and g == 0, "final": first or g > 0,
                "maxrow": last and g == 3 and arg == 0,
            }[kind]
            if not absent:
                uses[g, s] = (kind, arg, count)
                count += 1
    assert last or count % 2 == 0
    return uses, count


class Use:

    def __init__(self, number, batches_before, per_batch):
        self.bank = number % 2
        self.before = number // 2 + batches_before * (per_batch // 2)


def wait(eng, sem, value):
    if not isinstance(value, int) or value > 0:
        eng.wait_ge(sem, value)


def attention_ffn(nc, x, wq, wk, wv, wo, q_w, k_w, qweights, scales, biases, biases_t, lora_a, lora_b_t,
                  gamma_t, beta_t, cos, sin, identity, out):
    with ExitStack() as ctx:
        def sb(name, shape, dt=F32):
            return ctx.enter_context(nc.sbuf_tensor(name, shape, dt))

        def sem(name):
            return ctx.enter_context(nc.semaphore(name))

        xn_t = sb("xn_t", [P, B * L])
        xn_cur = sb("xn_cur", [P, L])
        w_qkv = sb("w_qkv", [P, KV, NPROJ])
        w_o = sb("w_o", [P, H // 2, D])
        ident = sb("ident", [P, P])
        cos_w = sb("cos_w", [P, NT, NQK])
        sin_w = sb("sin_w", [P, NT, NQK])
        raw = [sb(f"raw{i}", [P, NT, RAW]) for i in range(GROUPS)]
        squares = sb("squares", [P, NT, NQK])
        crossed = sb("crossed", [P, NT, NQK])
        rotated = [sb(f"rotated{i}", [P, NT, NQK]) for i in range(2)]
        ss = sb("ss", [P, NT * NV])
        sum_eps = sb("sum_eps", [P, NT * NV])
        rms_rs = sb("rms_rs", [P, NT * NV])
        minus_half = sb("minus_half", [P, NT * NV])
        rms_eps = sb("rms_eps", [P, NT * NV])
        ln_eps = sb("ln_eps", [P, NT])
        q_split = [sb(f"q_split{i}", [P, HG, L], F32R) for i in range(GROUPS)]
        q_hi = [sb(f"q_hi{i}", [P, HG, L], F32R) for i in range(GROUPS)]
        k_hi = [sb(f"k_hi{i}", [P, L], F32R) for i in range(GROUPS)]
        k_lo = [sb(f"k_lo{i}", [P, L], F32R) for i in range(GROUPS)]
        neg_max = [sb(f"neg_max{i}", [P, HG * NT]) for i in range(GROUPS)]
        max_row = [sb(f"max_row{i}", [8, P], F32R) for i in range(2)]
        probs = [sb(f"probs{i}", [P, NT, L]) for i in range(2)]
        inv_sum = [sb(f"inv_sum{i}", [P, NT]) for i in range(2)]
        o_tok = [sb(f"o_tok{i}", [P, NT, HG * DH]) for i in range(2)]
        o_t = sb("o_t", [P, 2, L])
        ln_stats = sb("ln_stats", [P, B * NT, 6])
        ln_mv = sb("ln_mv", [P, B * NT, 2])
        ln_var = sb("ln_var", [P, B * NT])
        ln_rs = sb("ln_rs", [P, B * NT])
        w_ffn = sb("w_ffn", [P, 2 * FB, D])
        bias_row = sb("bias_row", [P, FB, D])
        bias_col = sb("bias_col", [P, 2 * FB])
        gam = sb("gam", [P, FB])
        bet = sb("bet", [P, FB])
        h_all = sb("h", [P, FB + 1, L])
        h = [h_all[:, i, :] for i in range(FB + 1)]
        y_tok = sb("y_tok", [P, NT, D])
        f_stats = sb("f_stats", [P, NT, 6])
        f_mv = sb("f_mv", [P, NT, 2])
        f_var = sb("f_var", [P, NT])
        f_rs = sb("f_rs", [P, NT])
        y_t = sb("y_t", [P, L])
        out_tok = sb("out_tok", [P, NT, D])

        def bank(name):
            return ctx.enter_context(nc.psum_tensor(name, [P, 512], F32))

        score_ps = [bank(f"score_ps{i}") for i in range(2)]
        max_ps = [bank(f"max_ps{i}") for i in range(2)]
        pv_ps = [bank(f"pv_ps{i}") for i in range(2)]
        scratch_ps = [bank(f"scratch_ps{i}") for i in range(2)]

        x_in = [sem(f"x_in{b}") for b in range(B)]
        w_in = sem("w_in")
        w_o_in = sem("w_o_in")
        tab_in = sem("tab_in")
        ffn_in = sem("ffn_in")
        x_again = sem("x_again")
        out_stored = sem("out_stored")
        consts_set = sem("consts_set")
        tables_set = sem("tables_set")
        ln_stat = sem("ln_stat")
        ln_agg = sem("ln_agg")
        ln_varred = sem("ln_varred")
        ln_rsdone = sem("ln_rsdone")
        xn_tok_ready = sem("xn_tok_ready")
        xn_cur_ready = sem("xn_cur_ready")
        dve_step = sem("dve_step")
        deq = sem("deq")
        lora_ready = sem("lora_ready")
        h0_ready = sem("h0_ready")
        w_ffn_ready = sem("w_ffn_ready")
        scratch_full = [sem(f"scratch_full{i}") for i in range(2)]
        scratch_free = [sem(f"scratch_free{i}") for i in range(2)]
        squared = sem("squared")
        ss_ready = sem("ss_ready")
        pool_step = sem("pool_step")
        rotated_ready = sem("rotated_ready")
        hi_ready = sem("hi_ready")
        hi_copied = [sem(f"hi_copied{i}") for i in range(2)]
        max_full = sem("max_full")
        max_done = sem("max_done")
        max_placed = sem("max_placed")
        score_full = sem("score_full")
        exp_done = sem("exp_done")
        pv_full = sem("pv_full")
        inv_ready = sem("inv_ready")
        o_ready = sem("o_ready")
        streams_joined = sem("streams_joined")
        f_stat = sem("f_stat")
        f_agg = sem("f_agg")
        f_varred = sem("f_varred")
        f_rsdone = sem("f_rsdone")
        f_norm = sem("f_norm")

        x_tok = probs[0][:].rearrange("p a b -> p (a b)").rearrange("p (t d) -> p t d", d=D)
        xn_tok = x_tok
        spare = probs[1][:].rearrange("p a b -> p (a b)")
        q_int = spare[:, 0:768].bitcast(I32)
        cos_sb = spare[:, 768:1024].rearrange("p (t d) -> p t d", d=DH)
        sin_sb = spare[:, 1024:1280].rearrange("p (t d) -> p t d", d=DH)
        w_rep = spare[:, 1280:1600].rearrange("p (j d) -> p j d", d=DH)
        w_swap = spare[:, 1600:1920].rearrange("p (j d) -> p j d", d=DH)
        la, lb = (f.rearrange("p a b -> p (a b)")[0:R, 0:2 * FB * D].rearrange("r (i d) -> r i d", d=D)
                  for f in (o_tok[1][:], h_all[:, 2:4, :]))
        act_t = y_tok[:].rearrange("p t d -> p (t d)")
        deq_w = o_tok[0][:].rearrange("p a b -> p (a b)")[:, 0:2 * FB * D]
        scale_rep = o_t[:].rearrange("p a b -> p (a b)")[:, 0:2 * FB * D]

        PRO = [("xn_turn", 0)] + [("proj", 0, t) for t in range(NT)]
        PRO += [("proj", m, t) for m in (2, 1) for t in range(NT)] + [("turn", 0, j) for j in range(3)]
        PRO += [("maxrow", 0)] + [("turn", 1, j) for j in range(3)]
        PRO += [("xn_turn", b) for b in range(1, B)]
        pro = {use: Use(n, 0, 0) for n, use in enumerate(PRO)}
        kinds = {"first": batch_uses(True, False), "mid": batch_uses(False, False), "last": batch_uses(False, True)}
        per_first, per_mid, per_last = (kinds[k][1] for k in ("first", "mid", "last"))

        def use_at(kind, b, g, s):
            use = kinds[kind][0].get((g, s))
            if not use:
                return None
            number = len(PRO) + use[2] + (0 if kind == "first" else per_first)
            return use[0], use[1], Use(number, 0 if kind == "first" else b - 1, per_mid)

        def out_before(kind, b):
            tail = per_mid - kinds["mid"][0][3, 13][2]
            return Use(len(PRO) + per_first - tail, b - 1, per_mid)

        epi = [Use(len(PRO) + per_first + (B - 2) * per_mid + per_last + n, 0, 0) for n in range(4)]

        def full(eng, u):
            eng.wait_ge(scratch_full[u.bank], u.before + 1)
            return scratch_ps[u.bank]

        def read(eng, u):
            eng.wait_ge(scratch_free[u.bank], u.before + 1)

        def halves(ap):
            return ap.rearrange("p t (j s d) -> p t j s d", s=2, d=half)

        def batches(eng, body):
            body("first", 0)
            with eng.Fori(1, B - 1) as b:
                body("mid", b)
            body("last", B - 1)

        FFN_LOADS = 3 + D // QG + FB + 3
        half = DH // 2
        ALL = slice(None)
        block = ctx.enter_context(nc.Block())

        @block.sync
        def _(sp):
            def load(dst, src, s):
                sp.dma_start(dst, src).then_inc(s, 16)

            for b in range(B):
                load(x_tok[:, b * NT:(b + 1) * NT, :], x[b].rearrange("(t p) d -> p t d", p=P), x_in[b])
                if b == 0:
                    load(ident[:], identity, w_in)
                    load(w_qkv[:, :, 0:HG * DH], wq.rearrange("d (g n) -> d g n", g=KV), w_in)
                    load(w_qkv[:, :, HG * DH:NQK], wk.rearrange("d (g n) -> d g n", g=KV), w_in)
                    load(w_qkv[:, :, NQK:NPROJ], wv.rearrange("d (g n) -> d g n", g=KV), w_in)
                    load(cos_sb, cos.rearrange("(t p) d -> p t d", p=P), tab_in)
                    load(sin_sb, sin.rearrange("(t p) d -> p t d", p=P), tab_in)
                    for heads, w in ((slice(0, HG), q_w), (slice(HG, NV), k_w)):
                        n = heads.stop - heads.start
                        for dst, src in ((w_rep[:, heads, :], w), (w_swap[:, heads, 0:half], w[half:DH]),
                                         (w_swap[:, heads, half:DH], w[0:half])):
                            load(dst, src.partition_broadcast(n).partition_broadcast(P), tab_in)
            load(w_o[:], wo.rearrange("(c p) n -> p c n", p=P), w_o_in)

            def place_max(u, slot, part):
                read(sp, u)
                sp.dma_start(q_hi[slot][64:65, 2 * part:2 * part + 2, :].bitcast(F32),
                             max_row[part][:].bitcast(F32)).then_inc(max_placed, 16)

            def copy_hi(m, slot, pair):
                sp.wait_ge(hi_ready, m * 6 + 4 + 2 * pair)
                sp.dma_start(q_split[slot][0:64, 2 * pair:2 * pair + 2, :].bitcast(F32),
                             q_hi[slot][0:64, 2 * pair:2 * pair + 2, :].bitcast(F32)).then_inc(hi_copied[pair], 16)

            def body(kind, b):
                for g in range(GROUPS):
                    n = b * GROUPS + g
                    place_max(use_at(kind, b, g, 0)[2], g, 1)
                    if use_at(kind, b, g, 3):
                        copy_hi(n + 2, (g + 2) % GROUPS, 0)
                    if not (kind == "last" and g == 3):
                        place_max(use_at(kind, b, g, 9)[2], (g + 1) % GROUPS, 0)
                    if use_at(kind, b, g, 10):
                        copy_hi(n + 2, (g + 2) % GROUPS, 1)
                    if g == 1 and kind != "first":
                        read(sp, use_at(kind, b, 0, 15)[2])
                        dst = out[B - 2:B - 1] if kind == "last" else out[bass.ds(b - 1, 1)]
                        sp.dma_start(dst.rearrange("o (t p) d -> p (o t) d", p=P), out_tok[:]).then_inc(out_stored, 16)
                    if g == 3 and kind != "first":
                        sp.wait_ge(out_stored, 16 * b)
                        src = x[B - 1:B] if kind == "last" else x[bass.ds(b, 1)]
                        sp.dma_start(out_tok[:], src.rearrange("o (t p) d -> p (o t) d", p=P)).then_inc(x_again, 16)

            sp.dma_start(out_tok[:], x[0].rearrange("(t p) d -> p t d", p=P)).then_inc(x_again, 16)
            copy_hi(0, 0, 0)
            copy_hi(0, 0, 1)
            place_max(pro["maxrow", 0], 0, 0)
            copy_hi(1, 1, 0)
            copy_hi(1, 1, 1)
            batches(sp, body)
            read(sp, epi[3])
            sp.dma_start(out[B - 1].rearrange("(t p) d -> p t d", p=P), out_tok[:]).then_inc(out_stored, 16)
            sp.wait_ge(out_stored, 16 * B)

        @block.gpsimd
        def _(pool):
            for i in range(GROUPS):
                nc.gpsimd.memset(raw[i][:, :, NPROJ:RAW], 1.0)
            nc.gpsimd.memset(rms_eps[:], DH * RMS_EPS)
            nc.gpsimd.memset(ln_eps[:], LN_EPS)
            nc.gpsimd.memset(minus_half[:], -0.5).then_inc(consts_set, 1)
            pool.wait_ge(consts_set, 1)

            def layernorm_power(b):
                tiles = slice(b * NT, (b + 1) * NT)
                pool.wait_ge(ln_agg, b + 1)
                nc.gpsimd.tensor_tensor(ln_var[:, tiles], ln_mv[:, tiles, 1], ln_eps[:], ALU.add).then_inc(ln_varred, 1)
                pool.wait_ge(ln_varred, b + 1)
                nc.gpsimd.tensor_tensor(ln_rs[:, tiles], ln_var[:, tiles], minus_half[:, 0:NT],
                                        ALU.pow).then_inc(ln_rsdone, 1)

            def rms_power(m, steps):
                pool.wait_ge(ss_ready, m + 1)
                nc.gpsimd.tensor_tensor(sum_eps[:], ss[:], rms_eps[:], ALU.add).then_inc(pool_step, 1)
                pool.wait_ge(pool_step, steps + 1)
                nc.gpsimd.tensor_tensor(rms_rs[:], sum_eps[:], minus_half[:], ALU.pow).then_inc(pool_step, 1)

            layernorm_power(0)
            for b in range(1, B):
                layernorm_power(b)
            pool.wait_ge(tab_in, 16 * 8)
            for t in range(NT):
                for dst, tab, w in ((cos_w, cos_sb, w_rep), (sin_w, sin_sb, w_swap)):
                    nc.gpsimd.tensor_tensor(dst[:, t, :].rearrange("p (j d) -> p j d", d=DH), w,
                                            tab[:, t, :].unsqueeze(1).to_broadcast([P, NV, DH]),
                                            ALU.mult).then_inc(tables_set, 1)

            def rotate(m, last_two, slot, parity):
                r, dst = raw[slot], rotated[parity]
                steps = 4 + (m - 2) * 6
                for u in last_two:
                    read(pool, u)
                nc.gpsimd.tensor_tensor(squares[:], r[:, :, 0:NQK], r[:, :, 0:NQK], ALU.mult).then_inc(squared, 1)
                nc.gpsimd.tensor_tensor(dst[:], r[:, :, 0:NQK], cos_w[:], ALU.mult).then_inc(pool_step, 1)
                for s in range(2):
                    nc.gpsimd.tensor_tensor(halves(crossed[:])[:, :, :, s, :], halves(r[:, :, 0:NQK])[:, :, :, 1 - s, :],
                                            halves(sin_w[:])[:, :, :, s, :], ALU.mult).then_inc(pool_step, 1)
                rms_power(m, steps + 3)
                nc.gpsimd.tensor_tensor(dst[:], dst[:], crossed[:], ALU.add).then_inc(pool_step, 1)
                pool.wait_ge(pool_step, steps + 6)
                d3 = dst[:].rearrange("p t (j d) -> p (t j) d", d=DH)
                nc.gpsimd.tensor_tensor(d3, d3, rms_rs[:].unsqueeze(2).to_broadcast([P, NT * NV, DH]),
                                        ALU.mult).then_inc(rotated_ready, 1)

            rms_power(0, 0)
            pool.wait_ge(rotated_ready, 1)
            rms_power(1, 2)
            pool.wait_ge(rotated_ready, 2)
            rotate(2, (pro["proj", 2, NT - 2], pro["proj", 2, NT - 1]), 2, 0)

            def body(kind, b):
                for g in range(GROUPS):
                    n = b * GROUPS + g
                    if g < FB:
                        k = b * FB + g
                        pool.wait_ge(f_agg, k + 1)
                        nc.gpsimd.tensor_tensor(f_var[:], f_mv[:, :, 1], ln_eps[:], ALU.add).then_inc(f_varred, 1)
                        pool.wait_ge(f_varred, k + 1)
                        nc.gpsimd.tensor_tensor(f_rs[:], f_var[:], minus_half[:, 0:NT], ALU.pow).then_inc(f_rsdone, 1)
                    if use_at(kind, b, g, 7):
                        rotate(n + 3, (use_at(kind, b, g, 6)[2], use_at(kind, b, g, 7)[2]), (g + 3) % GROUPS, (g + 3) % 2)

            batches(pool, body)

        @block.scalar
        def _(act):
            def load(dst, src, s):
                act.dma_start(dst, src).then_inc(s, 16)

            load(q_int.rearrange("p (i o) -> p i o", o=D), qweights.rearrange("i d o -> d i o"), ffn_in)
            for q in range(D // QG):
                load(scale_rep[q * QG:(q + 1) * QG, :].rearrange("p (i o) -> p i o", o=D),
                     scales[:, q, :].partition_broadcast(QG), ffn_in)
            load(la, lora_a.rearrange("i r d -> r i d"), ffn_in)
            load(lb, lora_b_t.rearrange("i r o -> r i o"), ffn_in)
            for i in range(FB):
                load(bias_row[:, i, :], biases[2 * i].partition_broadcast(P), ffn_in)
            load(bias_col[:], biases_t, ffn_in)
            load(gam[:], gamma_t, ffn_in)
            load(bet[:], beta_t, ffn_in)

            def copy(u, dst, src):
                nc.scalar.activation(dst, full(act, u)[src], ACT.Copy).then_inc(scratch_free[u.bank], 1)

            def copy_raw(u, slot, t):
                copy(u, raw[slot][:, t, 0:NPROJ], (slice(None), slice(0, NPROJ)))

            def round_hi(u, slot, j):
                ps = full(act, u)
                for k in range(2):
                    if j == 0:
                        dst, src = k_hi[slot][64 * k:64 * k + 64, :], ps[64:128, :]
                    else:
                        dst, src = q_hi[slot][0:64, 2 * j - 2 + k, :], ps[64 * k:64 * k + 64, :]
                    nc.scalar.activation(dst, src, ACT.Copy).then_inc(hi_ready, 1)

            def copy_max(u, part, placed):
                wait(act, max_placed, placed)
                copy(u, max_row[part][:], (slice(0, 8), slice(0, P)))

            def exp(n, s):
                j = n * SLOTS + s
                if s % NT == 0:
                    wait(act, pv_full, n * HG + s // NT - 1)
                act.wait_ge(score_full, j + 1)
                nc.scalar.activation(probs[s // NT % 2][:, s % NT, :], score_ps[s % 2][:],
                                     ACT.Exp).then_inc(exp_done, 1)

            def square(m, last_two):
                wait(act, ss_ready, m)
                for u in last_two:
                    read(act, u)
                nc.scalar.activation(squares[:], raw[m][:, :, 0:NQK], ACT.Square).then_inc(squared, 1)

            for use in PRO:
                u = pro[use]
                if use[0] == "xn_turn":
                    copy(u, xn_t[:, use[1] * L:(use[1] + 1) * L], ALL)
                elif use[0] == "proj":
                    copy_raw(u, use[1], use[2])
                    if use[1] < 2 and use[2] == NT - 1:
                        square(use[1], [pro["proj", use[1], t] for t in (NT - 2, NT - 1)])
                elif use[0] == "turn":
                    round_hi(u, use[1], use[2])
                else:
                    copy_max(u, 0, 0)

            def body(kind, b):
                for g in range(GROUPS):
                    n = b * GROUPS + g
                    for s in range(SLOTS):
                        exp(n, s)
                        use = use_at(kind, b, g, s)
                        if not use:
                            continue
                        what, arg, u = use
                        if what == "proj":
                            copy_raw(u, (g + 3) % GROUPS, arg)
                        elif what == "turn":
                            round_hi(u, (g + 2) % GROUPS, arg)
                        elif what == "maxrow":
                            copy_max(u, arg, n * 32 + (0 if arg else 16))
                        elif what == "out_turn":
                            copy(u, o_t[:, arg, :], ALL)
                        elif what == "ffn_turn":
                            nc.scalar.activation(act_t, full(act, u)[:], ACT.Gelu, bias=bet[:, g:g + 1],
                                                 scale=gam[:, g:g + 1]).then_inc(scratch_free[u.bank], 1)
                        elif what == "out" and g == 1:
                            copy(u, y_t[:], ALL)

            batches(act, body)
            for pair in range(2):
                copy(epi[pair], o_t[:, pair, :], ALL)

        @block.tensor
        def _(pe):
            def begin(u):
                wait(pe, scratch_free[u.bank], u.before)
                return scratch_ps[u.bank]

            def turn4(u, tiles):
                ps = begin(u)
                for c in range(NT):
                    last = nc.tensor.transpose(ps[:, c * P:(c + 1) * P], tiles(c), ident[:])
                last.then_inc(scratch_full[u.bank], 1)

            def project(u, g, t):
                nc.tensor.matmul(begin(u)[:, 0:NPROJ], xn_cur[:, t * P:(t + 1) * P], w_qkv[:, g, :],
                                 start=True, stop=True).then_inc(scratch_full[u.bank], 1)

            def turn_heads(u, m, parity, j):
                pe.wait_ge(rotated_ready, m + 1)
                lo = NQK - P if j == 0 else (j - 1) * P
                turn4(u, lambda t: rotated[parity][:, t, lo:lo + P])

            def max_tile(m, slot, s, turned=()):
                if s % 8 == 0:
                    pe.wait_ge(hi_copied[s // 8], m * 16 + 16)
                    for u in turned:
                        read(pe, u)
                wait(pe, max_done, m * SLOTS + s - 1)
                nc.tensor.matmul(max_ps[s % 2][:], q_split[slot][:, s // NT, (s % NT) * P:(s % NT + 1) * P],
                                 k_hi[slot][:], start=True, stop=True).then_inc(max_full, 1)

            def max_row_turn(u, m, slot, part):
                pe.wait_ge(max_done, m * SLOTS + 8 * part + 8)
                nc.tensor.transpose(begin(u)[0:8, 0:P], neg_max[slot][:, 8 * part:8 * part + 8],
                                    ident[:]).then_inc(scratch_full[u.bank], 1)

            def score_tile(n, g, s):
                hd, c = s // NT, s % NT
                if c == 0 and hd % 2 == 0:
                    pe.wait_ge(max_placed, n * 32 + 16 + 8 * hd)
                wait(pe, exp_done, n * SLOTS + s - 1)
                keys = slice(c * P, (c + 1) * P)
                nc.tensor.matmul(score_ps[s % 2][:], k_hi[g][:, keys], q_split[g][:, hd, :], start=True, stop=False)
                nc.tensor.matmul(score_ps[s % 2][:], k_lo[g][0:65, keys], q_hi[g][0:65, hd, :], start=False,
                                 stop=True).then_inc(score_full, 1)

            def pv_tile(head, slot, hd, c):
                if c == 0:
                    pe.wait_ge(exp_done, head * NT + NT)
                    wait(pe, o_ready, head - 1)
                for kc in range(NT):
                    last = nc.tensor.matmul(pv_ps[hd % 2][:, c * 65:(c + 1) * 65],
                                            probs[hd % 2][:, kc, c * P:(c + 1) * P],
                                            raw[slot][:, kc, NQK:RAW], start=(kc == 0), stop=(kc == NT - 1))
                if c == NT - 1:
                    last.then_inc(pv_full, 1)

            def out_turn(u, heads, parity, pair):
                pe.wait_ge(o_ready, heads)
                turn4(u, lambda t: o_tok[parity][:, t, pair * P:(pair + 1) * P])

            def out_project(u, g, turned):
                for t in turned:
                    read(pe, t)
                ps = begin(u)
                for pair in range(2):
                    mm = nc.tensor.matmul(ps[:], w_o[:, 2 * g + pair, :], o_t[:, pair, :], start=(pair == 0),
                                          stop=(pair == 1))
                mm.then_inc(scratch_full[u.bank], 1)

            pe.wait_ge(w_in, 16 * 4)
            turned = [pro["turn", 0, j] for j in range(3)]
            for use in PRO:
                u = pro[use]
                if use[0] == "xn_turn":
                    pe.wait_ge(xn_tok_ready, use[1] + 1)
                    turn4(u, lambda t: xn_tok[:, use[1] * NT + t, :])
                elif use[0] == "proj":
                    pe.wait_ge(xn_cur_ready, 1)
                    project(u, use[1], use[2])
                elif use[0] == "maxrow":
                    for s in range(8):
                        max_tile(0, 0, s, turned)
                    max_row_turn(u, 0, 0, 0)
                else:
                    if use[1:] == (0, 0):
                        pe.wait_ge(ffn_in, 16 * FFN_LOADS)
                        for i in range(2 * FB):
                            mm = nc.tensor.matmul(pv_ps[i // 4][:, i % 4 * D:(i % 4 + 1) * D], la[:, i, :],
                                                  lb[:, i, :], start=True, stop=True)
                        mm.then_inc(lora_ready, 1)
                    turn_heads(u, use[1], use[1] % 2, use[2])
                    if use[1] == 1:
                        max_tile(0, 0, 8 + use[2], turned)
            for s in range(8 + 3, SLOTS):
                max_tile(0, 0, s, turned)
            pe.wait_ge(w_o_in, 16)

            def body(kind, b):
                for g in range(GROUPS):
                    n = b * GROUPS + g
                    for s in range(SLOTS):
                        score_tile(n, g, s)
                        use = use_at(kind, b, g, s)
                        what, arg, u = use or (None, None, None)
                        if what == "proj":
                            pe.wait_ge(xn_cur_ready, b + (1 if g == 0 else 2))
                            project(u, (g + 3) % GROUPS, arg)
                        elif what == "turn":
                            turn_heads(u, n + 2, g % 2, arg)
                        elif what == "maxrow" and arg == 1:
                            max_row_turn(u, n, g, 1)
                        elif what == "maxrow":
                            max_row_turn(u, n + 1, (g + 1) % GROUPS, 0)
                        elif what == "out_turn":
                            out_turn(u, n * HG, (g + 1) % 2, arg)
                        elif what == "out":
                            out_project(u, (g + 3) % GROUPS, [use_at(kind, b, g, t)[2] for t in (11, 12)])
                        elif what == "ffn1":
                            if g == 0:
                                pe.wait_ge(h0_ready, b + 1)
                                pe.wait_ge(w_ffn_ready, 1)
                            else:
                                read(pe, use_at(kind, b, g - 1, 14)[2])
                            ps = begin(u)
                            for t in range(NT):
                                mm = nc.tensor.matmul(ps[:, t * P:(t + 1) * P], h[g][:, t * P:(t + 1) * P],
                                                      w_ffn[:, 2 * g, :], start=True, stop=True)
                            mm.then_inc(scratch_full[u.bank], 1)
                        elif what == "ffn_turn":
                            pe.wait_ge(f_norm, b * FB + g + 1)
                            turn4(u, lambda t: y_tok[:, t, :])
                        elif what == "ffn2":
                            read(pe, use_at(kind, b, g, 8)[2])
                            nc.tensor.matmul(begin(u)[:], w_ffn[:, 2 * g + 1, :], act_t, start=True,
                                             stop=True).then_inc(scratch_full[u.bank], 1)
                        elif what == "final":
                            read(pe, use_at(kind, b, 0, 13)[2])
                            turn4(u, lambda t: y_t[:, t * P:(t + 1) * P])
                        if not (kind == "last" and g == 3):
                            max_tile(n + 1, (g + 1) % GROUPS, s)
                        hd = s // NT - 1
                        if hd >= 0:
                            pv_tile(n * HG + hd, g, hd, s % NT)
                        elif not (kind == "first" and g == 0):
                            pv_tile(n * HG - 1, (g + 3) % GROUPS, HG - 1, s % NT)

            batches(pe, body)

            for c in range(NT):
                pv_tile(B * H - 1, 3, HG - 1, c)
            for pair in range(2):
                out_turn(epi[pair], B * H, 1, pair)
            out_project(epi[2], 3, epi[0:2])
            read(pe, epi[2])
            turn4(epi[3], lambda t: y_t[:, t * P:(t + 1) * P])

        @block.vector
        def _(dve):
            def layernorm_x(b):
                tiles = range(b * NT, (b + 1) * NT)
                dve.wait_ge(x_in[b], 16)
                for t in tiles:
                    last = nc.vector.bn_stats(ln_stats[:, t, :], x_tok[:, t, :])
                last.then_inc(ln_stat, 1)
                dve.wait_ge(ln_stat, b + 1)
                for t in tiles:
                    last = nc.vector.bn_aggr(ln_mv[:, t, :], ln_stats[:, t, :])
                last.then_inc(ln_agg, 1)
                dve.wait_ge(ln_rsdone, b + 1)
                for t in tiles:
                    last = nc.vector.tensor_scalar(xn_tok[:, t, :], x_tok[:, t, :], ln_mv[:, t, 0:1],
                                                   ln_rs[:, t:t + 1], ALU.subtract, ALU.mult)
                last.then_inc(xn_tok_ready, 1)

            def sum_squares(m):
                dve.wait_ge(squared, m + 1)
                nc.vector.tensor_reduce(ss[:], squares[:].rearrange("p t (j d) -> p (t j) d", d=DH), AX.X,
                                        ALU.add).then_inc(ss_ready, 1)

            def split(u, m, slot, j):
                ps = full(dve, u)
                dve.wait_ge(hi_ready, m * 6 + 2 * j + 2)
                if j == 0:
                    last = nc.vector.tensor_tensor(k_lo[slot][0:64, :], ps[64:128, :],
                                                   k_hi[slot][0:64, :].bitcast(F32), ALU.subtract)
                else:
                    for k in range(2):
                        head = 2 * j - 2 + k
                        last = nc.vector.tensor_tensor(q_split[slot][64:128, head, :], ps[64 * k:64 * k + 64, :],
                                                       q_hi[slot][0:64, head, :].bitcast(F32), ALU.subtract)
                last.then_inc(scratch_free[u.bank], 1)

            def reduce_max(m, slot, s):
                dve.wait_ge(max_full, m * SLOTS + s + 1)
                nc.vector.tensor_reduce(neg_max[slot][:, s:s + 1], max_ps[s % 2][:], AX.X, ALU.max,
                                        negate=True).then_inc(max_done, 1)

            def normalise(head, hd, parity):
                dve.wait_ge(pv_full, head + 1)
                pv = pv_ps[hd % 2][:, 0:NT * 65].rearrange("p (c d) -> p c d", d=65)
                nc.vector.reciprocal(inv_sum[hd % 2][:], pv[:, :, DH]).then_inc(inv_ready, 1)
                dve.wait_ge(inv_ready, head + 1)
                nc.vector.tensor_tensor(o_tok[parity][:, :, hd * DH:(hd + 1) * DH], pv[:, :, 0:DH],
                                        inv_sum[hd % 2][:].unsqueeze(2).to_broadcast([P, NT, DH]),
                                        ALU.mult).then_inc(o_ready, 1)

            def add_out(u, before=None):
                if before:
                    read(dve, before)
                nc.vector.tensor_tensor(y_t[:], full(dve, u)[:], y_t[:], ALU.add).then_inc(scratch_free[u.bank], 1)

            def final_rows(u, b):
                dve.wait_ge(x_again, b * 16)
                rows = out_tok[:].rearrange("p t d -> p (t d)")
                nc.vector.tensor_tensor(rows, full(dve, u)[:], rows, ALU.add).then_inc(scratch_free[u.bank], 1)

            def rotate(m):
                r, dst = raw[m], rotated[m]
                nc.vector.tensor_tensor(dst[:], r[:, :, 0:NQK], cos_w[:], ALU.mult)
                for s in range(2):
                    last = nc.vector.tensor_tensor(
                        halves(crossed[:])[:, :, :, s, :], halves(r[:, :, 0:NQK])[:, :, :, 1 - s, :],
                        halves(sin_w[:])[:, :, :, s, :], ALU.mult)
                last.then_inc(dve_step, 1)
                dve.wait_ge(dve_step, 2 * m + 1)
                nc.vector.tensor_tensor(dst[:], dst[:], crossed[:], ALU.add).then_inc(dve_step, 1)
                dve.wait_ge(dve_step, 2 * m + 2)
                dve.wait_ge(pool_step, 2 * m + 2)
                d3 = dst[:].rearrange("p t (j d) -> p (t j) d", d=DH)
                nc.vector.tensor_tensor(d3, d3, rms_rs[:].unsqueeze(2).to_broadcast([P, NT * NV, DH]),
                                        ALU.mult).then_inc(rotated_ready, 1)

            for i in range(GROUPS):
                nc.vector.memset(k_lo[i][64:65, :].bitcast(F32), 1.0)
            layernorm_x(0)
            read(dve, pro["xn_turn", 0])
            nc.vector.tensor_copy(xn_cur[:], xn_t[:, 0:L]).then_inc(xn_cur_ready, 1)
            for b in range(1, B):
                layernorm_x(b)
            sum_squares(0)
            for u in (pro["proj", 0, NT - 2], pro["proj", 0, NT - 1]):
                read(dve, u)
            dve.wait_ge(tables_set, 2 * NT)
            rotate(0)
            dve.wait_ge(ffn_in, 16 * FFN_LOADS)
            nc.vector.tensor_scalar(deq_w, q_int, 1.0 / 7.5, -1.0, ALU.mult, ALU.add).then_inc(deq, 1)
            sum_squares(1)
            for j in range(3):
                split(pro["turn", 0, j], 0, 0, j)
            dve.wait_ge(deq, 1)
            nc.vector.tensor_tensor(deq_w, deq_w, scale_rep, ALU.mult).then_inc(deq, 1)
            for u in (pro["proj", 1, NT - 2], pro["proj", 1, NT - 1]):
                read(dve, u)
            rotate(1)
            for s in range(8):
                reduce_max(0, 0, s)
            for j in range(3):
                split(pro["turn", 1, j], 1, 1, j)
                reduce_max(0, 0, 8 + j)
            sum_squares(2)
            for s in range(8 + 3, SLOTS):
                reduce_max(0, 0, s)
            dve.wait_ge(deq, 2)
            dve.wait_ge(lora_ready, 1)
            w_flat = w_ffn[:].rearrange("p i o -> p (i o)")
            nc.vector.tensor_tensor(w_flat[:, 0:4 * D], deq_w[:, 0:4 * D], pv_ps[0][:], ALU.add)
            nc.vector.tensor_tensor(w_flat[:, 4 * D:6 * D], deq_w[:, 4 * D:6 * D], pv_ps[1][:, 0:2 * D],
                                    ALU.add).then_inc(w_ffn_ready, 1)

            def body(kind, b):
                for g in range(GROUPS):
                    n = b * GROUPS + g
                    for s in range(SLOTS):
                        if s % NT == 0 and not (kind == "first" and g == 0 and s < 8):
                            hd = s // NT - 2
                            normalise(n * HG + hd, hd % HG, g % 2 if hd >= 0 else (g + 1) % 2)
                        if g == 0 and s == 0:
                            nc.vector.tensor_copy(h[0], xn_t[:, bass.ds(b * L, L)] if kind == "mid" else
                                                  xn_t[:, b * L:(b + 1) * L]).then_inc(h0_ready, 1)
                        if g == 1 and s == 0 and kind != "last":
                            nc.vector.tensor_copy(xn_cur[:], xn_t[:, bass.ds((b + 1) * L, L)] if kind == "mid" else
                                                  xn_t[:, L:2 * L]).then_inc(xn_cur_ready, 1)
                        if g < FB and s == 4:
                            dve.wait_ge(f_rsdone, b * FB + g + 1)
                            for t in range(NT):
                                last = nc.vector.tensor_scalar(y_tok[:, t, :], y_tok[:, t, :], f_mv[:, t, 0:1],
                                                               f_rs[:, t:t + 1], ALU.subtract, ALU.mult)
                            last.then_inc(f_norm, 1)
                        if s == 12 and use_at(kind, b, g, 7):
                            sum_squares(n + 3)
                        what, arg, u = use_at(kind, b, g, s) or (None, None, None)
                        if what == "turn":
                            split(u, n + 2, (g + 2) % GROUPS, arg)
                        elif what == "ffn1":
                            k = b * FB + g + 1
                            nc.vector.tensor_tensor(y_tok[:], full(dve, u)[:].rearrange("p (t d) -> p t d", d=D),
                                                    bias_row[:, g, :].unsqueeze(1).to_broadcast([P, NT, D]),
                                                    ALU.add).then_inc(scratch_free[u.bank], 1)
                            read(dve, u)
                            for t in range(NT):
                                last = nc.vector.bn_stats(f_stats[:, t, :], y_tok[:, t, :])
                            last.then_inc(f_stat, 1)
                        elif what == "ffn2":
                            nc.vector.scalar_tensor_tensor(
                                out=h[g + 1], in0=full(dve, u)[:], scalar=bias_col[:, 2 * g + 1:2 * g + 2],
                                in1=h[g], op0=ALU.add, op1=ALU.add).then_inc(scratch_free[u.bank], 1)
                        elif what == "final":
                            final_rows(u, b)
                        elif what == "out" and g == 2:
                            add_out(u, use_at(kind, b, 1, 13)[2])
                        elif what == "out" and g == 3:
                            dve.wait_ge(streams_joined, b + 1)
                            add_out(u)
                        elif what == "out" and g == 0:
                            add_out(u, out_before(kind, b))
                        if g == 2 and s == 15:
                            read(dve, use_at(kind, b, 2, 13)[2])
                            read(dve, use_at(kind, b, 2, 14)[2])
                            nc.vector.tensor_tensor(y_t[:], y_t[:], h[FB], ALU.add).then_inc(streams_joined, 1)
                        if what == "ffn1":
                            dve.wait_ge(f_stat, k)
                        if not (kind == "last" and g == 3):
                            reduce_max(n + 1, (g + 1) % GROUPS, s)
                        if what == "ffn1":
                            for t in range(NT):
                                last = nc.vector.bn_aggr(f_mv[:, t, :], f_stats[:, t, :])
                            last.then_inc(f_agg, 1)

            batches(dve, body)
            for head in (B * H - 2, B * H - 1):
                normalise(head, head % HG, 1)
            add_out(epi[2])
            final_rows(epi[3], B)


def kernel(**inputs):
    import concourse.bacc as bacc
    from concourse.bass_utils import run_bass_kernel_spmd

    given = {name.replace("L0_", ""): np.asarray(a) for name, a in inputs.items()}
    t = np.ascontiguousarray

    inv_freq = (1.0 / 10000.0 ** (np.arange(0, DH, 2, dtype=np.float32) / DH)).astype(np.float32)
    freqs = np.arange(L - 1, dtype=np.float32)[:, None] * inv_freq[None, :]
    cos, sin = np.ones((L, DH), np.float32), np.zeros((L, DH), np.float32)
    cos[1:] = np.cos(np.concatenate([freqs, freqs], 1))
    sin[1:] = np.concatenate([-np.sin(freqs), np.sin(freqs)], 1)

    arrays = {
        "x": t(given["attn_inputs"]),
        "wq": t(given["attn_Wq"].T), "wk": t(given["attn_Wk"].T), "wv": t(given["attn_Wv"].T),
        "wo": t(given["attn_Wo"].T),
        "q_w": t(given["attn_q_norm_w"]), "k_w": t(given["attn_k_norm_w"]),
        "qweights": t(given["ffn_qweights"].transpose(0, 2, 1)), "scales": t(given["ffn_scales"].transpose(0, 2, 1)),
        "biases": t(given["ffn_biases"]), "biases_t": t(given["ffn_biases"].T),
        "lora_a": t(given["ffn_lora_a"]), "lora_b_t": t(given["ffn_lora_b"].transpose(0, 2, 1)),
        "gamma_t": t(given["ffn_ln_gamma"].T), "beta_t": t(given["ffn_ln_beta"].T),
        "cos": cos * np.float32(DH ** 0.5), "sin": sin * np.float32(DH ** 0.5), "identity": np.eye(P, dtype=np.float32),
    }
    nc = bacc.Bacc("TRN2", target_bir_lowering=False, num_devices=1)
    aps = {name: nc.dram_tensor(name, a.shape, mybir.dt.from_np(a.dtype), kind="ExternalInput").ap()
           for name, a in arrays.items()}
    out = nc.dram_tensor("out", (B, L, D), F32, kind="ExternalOutput").ap()
    attention_ffn(nc, out=out, **aps)
    result = run_bass_kernel_spmd(nc, [arrays], core_ids=[0])
    return result.results[0]["out"]
```

```python
from contextlib import ExitStack

import numpy as np

import concourse.bass as bass
from concourse import mybir
from concourse.alu_op_type import AluOpType as ALU

F32 = mybir.dt.float32
F32R = mybir.dt.float32r
I32 = mybir.dt.int32
ACT = mybir.ActivationFunctionType
AX = mybir.AxisListType

B, L, D = 4, 512, 128
P = 128
NT = L // P
H, KV, DH = 16, 4, 64
HG = H // KV
NV = HG + 1
NQK = NV * DH
NPROJ = NQK + DH
RAW = NPROJ + 1
FB, R, QG = 3, 32, 16
LN_EPS, RMS_EPS = 1e-5, 1e-6
SLOTS = 16
GROUPS = 4

SCRATCH = {0: ("maxrow", 1), 1: ("ffn1", 0), 2: ("turn", 0), 3: ("turn", 1), 4: ("proj", 0), 5: ("proj", 1),
           6: ("proj", 2), 7: ("proj", 3), 8: ("ffn_turn", 0), 9: ("maxrow", 0), 10: ("turn", 2),
           11: ("out_turn", 0), 12: ("out_turn", 1), 13: ("out", 0), 14: ("ffn2", 0), 15: ("final", 0)}

STEP_0 = {0: ("turn_1", 0), 1: ("ffn1", 0), 2: ("turn_1", 1), 3: ("turn_1", 2), 4: ("maxrow", 1), 5: ("proj", 0),
          6: ("proj", 1), 7: ("proj", 2), 8: ("proj", 3), 9: ("ffn_turn", 0), 10: ("turn", 0), 11: ("maxrow", 0),
          12: ("turn", 1), 13: ("turn", 2), 14: ("ffn2", 0), 15: ("xn_turn", 1)}
STEP_0_MAX = {s: [(0, 12 + 2 * s), (0, 13 + 2 * s)] for s in range(2)}
STEP_0_BUSY = {1: 2, 2: 3, 3: 2, 4: 4}
STEP_0_MAX.update({s: [(1, 2 * s - 10), (1, 2 * s - 9)] for s in range(5, 13)})


def batch_uses(first, last):
    uses, count = {}, 0
    for g in range(GROUPS):
        for s in range(SLOTS):
            step_0 = first and g == 0
            kind, arg = STEP_0[s] if step_0 else SCRATCH[s]
            if first and s == 15 and g in (1, 2):
                kind, arg = "xn_turn", g + 1
            absent = {
                "ffn1": g == FB, "ffn_turn": g == FB, "ffn2": g == FB,
                "turn": last and g >= 2, "proj": last and g >= 1, "final": first or g > 0,
                "maxrow": last and g == 3 and arg == 0,
            }.get(kind, False)
            if not absent:
                uses[g, s] = (kind, arg, count)
                count += 1
    assert first or last or count % 2 == 0
    return uses, count


class Use:

    def __init__(self, number, batches_before, per_batch):
        self.bank = number % 2
        self.before = number // 2 + batches_before * (per_batch // 2)


def wait(eng, sem, value):
    if not isinstance(value, int) or value > 0:
        eng.wait_ge(sem, value)


def attention_ffn(nc, x, wq, wk, wv, wo, q_w, k_w, qweights, scales, biases, biases_t, lora_a, lora_b_t,
                  gamma_t, beta_t, cos, sin, identity, out):
    with ExitStack() as ctx:
        def sb(name, shape, dt=F32):
            return ctx.enter_context(nc.sbuf_tensor(name, shape, dt))

        def sem(name):
            return ctx.enter_context(nc.semaphore(name))

        xn_t = sb("xn_t", [P, B * L])
        xn_hi = sb("xn_hi", [P, L], F32R)
        xn_lo = sb("xn_lo", [P, L], F32R)
        w_hi = sb("w_hi", [P, KV, NPROJ], F32R)
        w_lo = sb("w_lo", [P, KV, NPROJ], F32R)
        w_o = sb("w_o", [P, H // 2, D])
        ident = sb("ident", [P, P])
        cos_w = sb("cos_w", [P, NT, NQK])
        sin_w = sb("sin_w", [P, NT, NQK])
        raw = [sb(f"raw{i}", [P, NT, RAW]) for i in range(GROUPS)]
        crossed = sb("crossed", [P, NT, NQK])
        rotated = [sb(f"rotated{i}", [P, NT, NQK]) for i in range(2)]
        ss = sb("ss", [P, NT * NV])
        sum_eps = sb("sum_eps", [P, NT * NV])
        rms_rs = sb("rms_rs", [P, NT * NV])
        minus_half = sb("minus_half", [P, NT * NV])
        rms_eps = sb("rms_eps", [P, NT * NV])
        early_ss = sb("early_ss", [P, NT * NV])
        early_sum_eps = sb("early_sum_eps", [P, NT * NV])
        early_rs = sb("early_rs", [P, NT * NV])
        ln_eps = sb("ln_eps", [P, B * NT])
        q_split = [sb(f"q_split{i}", [P, HG, L], F32R) for i in range(GROUPS)]
        q_hi = [sb(f"q_hi{i}", [P, HG, L], F32R) for i in range(GROUPS)]
        k_hi = [sb(f"k_hi{i}", [P, L], F32R) for i in range(GROUPS)]
        k_lo = [sb(f"k_lo{i}", [P, L], F32R) for i in range(GROUPS)]
        neg_max = [sb(f"neg_max{i}", [P, HG * NT]) for i in range(GROUPS)]
        max_row = [sb(f"max_row{i}", [8, P], F32R) for i in range(2)]
        probs = [sb(f"probs{i}", [P, NT, L]) for i in range(2)]
        inv_sum = [sb(f"inv_sum{i}", [P, NT]) for i in range(2)]
        o_tok = [sb(f"o_tok{i}", [P, NT, HG * DH]) for i in range(2)]
        o_t = sb("o_t", [P, 2, L])
        ln_stats = sb("ln_stats", [P, B * NT, 6])
        ln_mv = sb("ln_mv", [P, B * NT, 2])
        ln_var = sb("ln_var", [P, B * NT])
        ln_rs = sb("ln_rs", [P, B * NT])
        w_ffn = sb("w_ffn", [P, 2 * FB, D])
        bias_row = sb("bias_row", [P, FB, D])
        bias_col = sb("bias_col", [P, 2 * FB])
        gam = sb("gam", [P, FB])
        bet = sb("bet", [P, FB])
        h_all = sb("h", [P, FB + 1, L])
        h = [h_all[:, i, :] for i in range(FB + 1)]
        y_tok = sb("y_tok", [P, NT, D])
        f_stats = sb("f_stats", [P, NT, 6])
        f_mv = sb("f_mv", [P, NT, 2])
        f_var = sb("f_var", [P, NT])
        f_rs = sb("f_rs", [P, NT])
        y_t = sb("y_t", [P, L])
        out_tok = sb("out_tok", [P, NT, D])

        def bank(name):
            return ctx.enter_context(nc.psum_tensor(name, [P, 512], F32))

        score_ps = [bank(f"score_ps{i}") for i in range(2)]
        max_ps = [bank(f"max_ps{i}") for i in range(2)]
        pv_ps = [bank(f"pv_ps{i}") for i in range(2)]
        scratch_ps = [bank(f"scratch_ps{i}") for i in range(2)]

        x_in = [sem(f"x_in{b}") for b in range(B)]
        w_in = sem("w_in")
        w_o_in = sem("w_o_in")
        tab_in = sem("tab_in")
        ffn_in = sem("ffn_in")
        out_stored = sem("out_stored")
        consts_set = sem("consts_set")
        tables_set = sem("tables_set")
        ln_stat = sem("ln_stat")
        ln_agg = sem("ln_agg")
        ln_varred = sem("ln_varred")
        ln_rsdone = sem("ln_rsdone")
        xn_tok_ready = sem("xn_tok_ready")
        xn_hi_ready = sem("xn_hi_ready")
        xn_cur_ready = sem("xn_cur_ready")
        w_hi_ready = sem("w_hi_ready")
        w_lo_ready = sem("w_lo_ready")
        dve_step = sem("dve_step")
        deq = sem("deq")
        lora_ready = sem("lora_ready")
        h0_ready = sem("h0_ready")
        w_ffn_ready = sem("w_ffn_ready")
        scratch_full = [sem(f"scratch_full{i}") for i in range(2)]
        scratch_free = [sem(f"scratch_free{i}") for i in range(2)]
        squared = sem("squared")
        ss_ready = sem("ss_ready")
        x_again = sem("x_again")
        early_squared = sem("early_squared")
        early_ss_ready = sem("early_ss_ready")
        early_rms = sem("early_rms")
        pool_step = sem("pool_step")
        rotated_ready = sem("rotated_ready")
        hi_ready = sem("hi_ready")
        hi_copied = [sem(f"hi_copied{i}") for i in range(2)]
        max_full = sem("max_full")
        max_done = sem("max_done")
        max_placed = sem("max_placed")
        score_full = sem("score_full")
        exp_done = sem("exp_done")
        pv_full = sem("pv_full")
        inv_ready = sem("inv_ready")
        o_ready = sem("o_ready")
        streams_joined = sem("streams_joined")
        f_stat = sem("f_stat")
        f_agg = sem("f_agg")
        f_varred = sem("f_varred")
        f_rsdone = sem("f_rsdone")
        f_norm = sem("f_norm")

        x_tok = [f.rearrange("p (t d) -> p t d", d=D) for f in (y_t[:], h[2], h[3], out_tok[:].rearrange("p t d -> p (t d)"))]
        early_crossed = raw[3][:, :, 0:NQK]
        w_qkv = xn_t[:, L:4 * L].rearrange("p (g n) -> p g n", g=KV)
        probs0 = probs[0][:].rearrange("p a b -> p (a b)")
        early_squares = probs0[:, 0:NT * NQK].rearrange("p (t n) -> p t n", n=NQK)
        spare = probs[1][:].rearrange("p a b -> p (a b)")
        q_int = spare[:, 0:768].bitcast(I32)
        cos_sb = spare[:, 768:1024].rearrange("p (t d) -> p t d", d=DH)
        sin_sb = spare[:, 1024:1280].rearrange("p (t d) -> p t d", d=DH)
        w_rep = spare[:, 1280:1600].rearrange("p (j d) -> p j d", d=DH)
        w_swap = spare[:, 1600:1920].rearrange("p (j d) -> p j d", d=DH)
        la, lb = (f[0:R, :].rearrange("r (i d) -> r i d", d=D)
                  for f in (o_tok[1][:].rearrange("p a b -> p (a b)")[:, 0:2 * FB * D], probs0[:, NT * NQK:]))
        act_t = y_tok[:].rearrange("p t d -> p (t d)")
        deq_w = o_tok[0][:].rearrange("p a b -> p (a b)")[:, 0:2 * FB * D]
        scale_rep = o_t[:].rearrange("p a b -> p (a b)")[:, 0:2 * FB * D]

        PRO = [("xn_turn", 0)] + [("proj", 0, t) for t in range(NT)]
        PRO += [("proj", m, t) for m in (1, 2) for t in range(NT)] + [("turn", 0, j) for j in range(3)]
        PRO += [("maxrow", 0)]
        pro = {use: Use(n, 0, 0) for n, use in enumerate(PRO)}
        kinds = {"first": batch_uses(True, False), "mid": batch_uses(False, False), "last": batch_uses(False, True)}
        per_first, per_mid, per_last = (kinds[k][1] for k in ("first", "mid", "last"))

        def use_at(kind, b, g, s):
            use = kinds[kind][0].get((g, s))
            if not use:
                return None
            number = len(PRO) + use[2] + (0 if kind == "first" else per_first)
            return use[0], use[1], Use(number, 0 if kind == "first" else b - 1, per_mid)

        def out_before(kind, b):
            tail = per_mid - kinds["mid"][0][3, 13][2]
            return Use(len(PRO) + per_first - tail, b - 1, per_mid)

        epi = [Use(len(PRO) + per_first + (B - 2) * per_mid + per_last + n, 0, 0) for n in range(4)]

        def full(eng, u):
            eng.wait_ge(scratch_full[u.bank], u.before + 1)
            return scratch_ps[u.bank]

        def read(eng, u):
            eng.wait_ge(scratch_free[u.bank], u.before + 1)

        def halves(ap):
            return ap.rearrange("p t (j s d) -> p t j s d", s=2, d=half)

        def batches(eng, body):
            body("first", 0)
            with eng.Fori(1, B - 1) as b:
                body("mid", b)
            body("last", B - 1)

        FFN_LOADS = 3 + D // QG + FB + 3
        half = DH // 2
        ALL = slice(None)
        block = ctx.enter_context(nc.Block())

        @block.sync
        def _(sp):
            def load(dst, src, s):
                sp.dma_start(dst, src).then_inc(s, 16)

            for b in range(B):
                load(x_tok[b], x[b].rearrange("(t p) d -> p t d", p=P), x_in[b])
                if b == 0:
                    load(ident[:], identity, w_in)
                    load(w_qkv[:, :, 0:HG * DH], wq.rearrange("d (g n) -> d g n", g=KV), w_in)
                    load(w_qkv[:, :, HG * DH:NQK], wk.rearrange("d (g n) -> d g n", g=KV), w_in)
                    load(w_qkv[:, :, NQK:NPROJ], wv.rearrange("d (g n) -> d g n", g=KV), w_in)
                    load(cos_sb, cos.rearrange("(t p) d -> p t d", p=P), tab_in)
                    load(sin_sb, sin.rearrange("(t p) d -> p t d", p=P), tab_in)
                    for heads, w in ((slice(0, HG), q_w), (slice(HG, NV), k_w)):
                        n = heads.stop - heads.start
                        for dst, src in ((w_rep[:, heads, :], w), (w_swap[:, heads, 0:half], w[half:DH]),
                                         (w_swap[:, heads, half:DH], w[0:half])):
                            load(dst, src.partition_broadcast(n).partition_broadcast(P), tab_in)
            load(q_int.rearrange("p (i o) -> p i o", o=D), qweights.rearrange("i d o -> d i o"), ffn_in)
            for q in range(D // QG):
                load(scale_rep[q * QG:(q + 1) * QG, :].rearrange("p (i o) -> p i o", o=D),
                     scales[:, q, :].partition_broadcast(QG), ffn_in)
            load(la, lora_a.rearrange("i r d -> r i d"), ffn_in)
            load(lb, lora_b_t.rearrange("i r o -> r i o"), ffn_in)
            for i in range(FB):
                load(bias_row[:, i, :], biases[2 * i].partition_broadcast(P), ffn_in)
            load(bias_col[:], biases_t, ffn_in)
            load(gam[:], gamma_t, ffn_in)
            load(bet[:], beta_t, ffn_in)
            load(w_o[:], wo.rearrange("(c p) n -> p c n", p=P), w_o_in)

            def place_max(u, slot, part):
                read(sp, u)
                sp.dma_start(q_hi[slot][64:65, 2 * part:2 * part + 2, :].bitcast(F32),
                             max_row[part][:].bitcast(F32)).then_inc(max_placed, 16)

            def copy_hi(m, slot, pair):
                sp.wait_ge(hi_ready, m * 6 + 4 + 2 * pair)
                sp.dma_start(q_split[slot][0:64, 2 * pair:2 * pair + 2, :].bitcast(F32),
                             q_hi[slot][0:64, 2 * pair:2 * pair + 2, :].bitcast(F32)).then_inc(hi_copied[pair], 16)

            def slot(kind, b, g, s):
                return use_at(kind, b, g, s)[2]

            def body(kind, b):
                for g in range(GROUPS):
                    n = b * GROUPS + g
                    if kind == "first" and g == 0:
                        copy_hi(1, 1, 0)
                        copy_hi(1, 1, 1)
                        place_max(slot(kind, b, 0, 4), 0, 1)
                        place_max(slot(kind, b, 0, 11), 1, 0)
                        copy_hi(2, 2, 0)
                        copy_hi(2, 2, 1)
                        continue
                    place_max(slot(kind, b, g, 0), g, 1)
                    if use_at(kind, b, g, 3):
                        copy_hi(n + 2, (g + 2) % GROUPS, 0)
                    if not (kind == "last" and g == 3):
                        place_max(slot(kind, b, g, 9), (g + 1) % GROUPS, 0)
                    if use_at(kind, b, g, 10):
                        copy_hi(n + 2, (g + 2) % GROUPS, 1)
                    if g == 1 and kind != "first":
                        read(sp, slot(kind, b, 0, 15))
                        dst = out[B - 2:B - 1] if kind == "last" else out[bass.ds(b - 1, 1)]
                        sp.dma_start(dst.rearrange("o (t p) d -> p (o t) d", p=P), out_tok[:]).then_inc(out_stored, 16)
                    if g == 3:
                        if kind == "first":
                            read(sp, slot(kind, b, 2, 15))
                        else:
                            sp.wait_ge(out_stored, 16 * b)
                        src = x[bass.ds(b, 1)] if kind == "mid" else x[b:b + 1]
                        sp.dma_start(out_tok[:], src.rearrange("o (t p) d -> p (o t) d", p=P)).then_inc(x_again, 16)

            copy_hi(0, 0, 0)
            copy_hi(0, 0, 1)
            place_max(pro["maxrow", 0], 0, 0)
            batches(sp, body)
            read(sp, epi[3])
            sp.dma_start(out[B - 1].rearrange("(t p) d -> p t d", p=P), out_tok[:]).then_inc(out_stored, 16)
            sp.wait_ge(out_stored, 16 * B)

        @block.gpsimd
        def _(pool):
            for i in range(GROUPS):
                nc.gpsimd.memset(raw[i][:, :, NPROJ:RAW], 1.0)
            nc.gpsimd.memset(rms_eps[:], DH * RMS_EPS)
            nc.gpsimd.memset(ln_eps[:], LN_EPS)
            nc.gpsimd.memset(minus_half[:], -0.5).then_inc(consts_set, 1)
            pool.wait_ge(consts_set, 1)

            def layernorm_power(call, count, tiles):
                pool.wait_ge(ln_agg, count)
                nc.gpsimd.tensor_tensor(ln_var[:, tiles], ln_mv[:, tiles, 1], ln_eps[:, tiles],
                                        ALU.add).then_inc(ln_varred, 1)
                pool.wait_ge(ln_varred, call)
                nc.gpsimd.tensor_tensor(ln_rs[:, tiles], ln_var[:, tiles], minus_half[:, 0:tiles.stop - tiles.start],
                                        ALU.pow).then_inc(ln_rsdone, 1)

            layernorm_power(1, 1, slice(0, NT))
            pool.wait_ge(early_ss_ready, 1)
            nc.gpsimd.tensor_tensor(early_sum_eps[:], early_ss[:], rms_eps[:], ALU.add).then_inc(early_rms, 1)
            pool.wait_ge(early_rms, 1)
            nc.gpsimd.tensor_tensor(early_rs[:], early_sum_eps[:], minus_half[:], ALU.pow).then_inc(early_rms, 1)
            pool.wait_ge(tables_set, 2 * NT)

            def rotate(m, last_two, slot, parity, turned=(), between=None):
                r, dst = raw[slot], rotated[parity]
                steps = (m - 1) * 6
                for u in last_two:
                    read(pool, u)
                for u in turned:
                    full(pool, u)
                nc.gpsimd.tensor_tensor(dst[:], r[:, :, 0:NQK], r[:, :, 0:NQK], ALU.mult).then_inc(squared, 1)
                for s in range(2):
                    nc.gpsimd.tensor_tensor(halves(crossed[:])[:, :, :, s, :], halves(r[:, :, 0:NQK])[:, :, :, 1 - s, :],
                                            halves(sin_w[:])[:, :, :, s, :], ALU.mult).then_inc(pool_step, 1)
                pool.wait_ge(ss_ready, m)
                nc.gpsimd.tensor_tensor(sum_eps[:], ss[:], rms_eps[:], ALU.add).then_inc(pool_step, 1)
                nc.gpsimd.tensor_tensor(dst[:], r[:, :, 0:NQK], cos_w[:], ALU.mult).then_inc(pool_step, 1)
                if between:
                    between()
                pool.wait_ge(pool_step, steps + 4)
                nc.gpsimd.tensor_tensor(rms_rs[:], sum_eps[:], minus_half[:], ALU.pow).then_inc(pool_step, 1)
                nc.gpsimd.tensor_tensor(dst[:], dst[:], crossed[:], ALU.add).then_inc(pool_step, 1)
                pool.wait_ge(pool_step, steps + 6)
                d3 = dst[:].rearrange("p t (j d) -> p (t j) d", d=DH)
                nc.gpsimd.tensor_tensor(d3, d3, rms_rs[:].unsqueeze(2).to_broadcast([P, NT * NV, DH]),
                                        ALU.mult).then_inc(rotated_ready, 1)

            def ffn_power(k):
                pool.wait_ge(f_agg, k + 1)
                nc.gpsimd.tensor_tensor(f_var[:], f_mv[:, :, 1], ln_eps[:, 0:NT], ALU.add).then_inc(f_varred, 1)
                pool.wait_ge(f_varred, k + 1)
                nc.gpsimd.tensor_tensor(f_rs[:], f_var[:], minus_half[:, 0:NT], ALU.pow).then_inc(f_rsdone, 1)

            rotate(1, (pro["proj", 1, NT - 2], pro["proj", 1, NT - 1]), 1, 1)
            rotate(2, (pro["proj", 2, NT - 2], pro["proj", 2, NT - 1]), 2, 0, [pro["turn", 0, j] for j in (1, 2)],
                   between=lambda: ffn_power(0))
            layernorm_power(2, 2, slice(NT, B * NT))

            def body(kind, b):
                for g in range(GROUPS):
                    n = b * GROUPS + g
                    step_0 = kind == "first" and g == 0
                    if g < FB and not step_0:
                        ffn_power(b * FB + g)
                    proj = (7, 8) if step_0 else (6, 7)
                    if use_at(kind, b, g, 7):
                        rotate(n + 3, [use_at(kind, b, g, s)[2] for s in proj], (g + 3) % GROUPS, (g + 3) % 2)

            batches(pool, body)

        @block.scalar
        def _(act):
            def copy(u, dst, src):
                nc.scalar.activation(dst, full(act, u)[src], ACT.Copy).then_inc(scratch_free[u.bank], 1)

            def copy_raw(u, slot, t):
                copy(u, raw[slot][:, t, 0:NPROJ], (slice(None), slice(0, NPROJ)))

            def round_hi(u, slot, j):
                ps = full(act, u)
                for k in range(2):
                    if j == 0:
                        dst, src = k_hi[slot][64 * k:64 * k + 64, :], ps[64:128, :]
                    else:
                        dst, src = q_hi[slot][0:64, 2 * j - 2 + k, :], ps[64 * k:64 * k + 64, :]
                    nc.scalar.activation(dst, src, ACT.Copy).then_inc(hi_ready, 1)

            def copy_max(u, part, placed):
                wait(act, max_placed, placed)
                copy(u, max_row[part][:], (slice(0, 8), slice(0, P)))

            def exp(n, s):
                j = n * SLOTS + s
                if s % NT == 0:
                    wait(act, pv_full, n * HG + s // NT - 1)
                act.wait_ge(score_full, j + 1)
                nc.scalar.activation(probs[s // NT % 2][:, s % NT, :], score_ps[s % 2][:],
                                     ACT.Exp).then_inc(exp_done, 1)

            def square(m, last_two):
                for u in last_two:
                    read(act, u)
                nc.scalar.activation(early_squares, raw[m][:, :, 0:NQK], ACT.Square).then_inc(early_squared, 1)

            def round_w(g):
                nc.scalar.activation(w_hi[:, g, :], w_qkv[:, g, :], ACT.Copy).then_inc(w_hi_ready, 1)

            act.wait_ge(w_in, 16 * 4)
            round_w(0)
            for use in PRO:
                u = pro[use]
                if use[0] == "xn_turn":
                    nc.scalar.activation(xn_hi[:], full(act, u)[:], ACT.Copy).then_inc(xn_hi_ready, 1)
                    copy(u, xn_t[:, 0:L], ALL)
                    for g in range(1, KV):
                        round_w(g)
                elif use[0] == "proj":
                    copy_raw(u, use[1], use[2])
                    if use[1] == 0 and use[2] == NT - 1:
                        square(use[1], [pro["proj", use[1], t] for t in (NT - 2, NT - 1)])
                elif use[0] == "turn":
                    round_hi(u, use[1], use[2])
                else:
                    copy_max(u, 0, 0)

            def body(kind, b):
                for g in range(GROUPS):
                    n = b * GROUPS + g
                    for s in range(SLOTS):
                        exp(n, s)
                        if g == 1 and s == 0 and kind != "last":
                            if kind == "first":
                                read(act, use_at(kind, b, 0, 15)[2])
                            nc.scalar.activation(xn_hi[:], xn_t[:, bass.ds((b + 1) * L, L)] if kind == "mid" else
                                                 xn_t[:, L:2 * L], ACT.Copy).then_inc(xn_hi_ready, 1)
                        use = use_at(kind, b, g, s)
                        if not use:
                            continue
                        what, arg, u = use
                        if what == "proj":
                            copy_raw(u, (g + 3) % GROUPS, arg)
                        elif what == "turn":
                            round_hi(u, (g + 2) % GROUPS, arg)
                        elif what == "turn_1":
                            round_hi(u, 1, arg)
                        elif what == "maxrow":
                            copy_max(u, arg, n * 32 + (0 if arg else 16))
                        elif what == "out_turn":
                            copy(u, o_t[:, arg, :], ALL)
                        elif what == "ffn_turn":
                            nc.scalar.activation(act_t, full(act, u)[:], ACT.Gelu, bias=bet[:, g:g + 1],
                                                 scale=gam[:, g:g + 1]).then_inc(scratch_free[u.bank], 1)
                        elif what == "xn_turn":
                            copy(u, xn_t[:, arg * L:(arg + 1) * L], ALL)
                        elif what == "out" and g == 1:
                            copy(u, y_t[:], ALL)

            batches(act, body)
            for pair in range(2):
                copy(epi[pair], o_t[:, pair, :], ALL)

        @block.tensor
        def _(pe):
            def begin(u):
                wait(pe, scratch_free[u.bank], u.before)
                return scratch_ps[u.bank]

            def turn4(u, tiles):
                ps = begin(u)
                for c in range(NT):
                    last = nc.tensor.transpose(ps[:, c * P:(c + 1) * P], tiles(c), ident[:])
                last.then_inc(scratch_full[u.bank], 1)

            def project(u, g, t):
                ps, rows = begin(u)[:, 0:NPROJ], slice(t * P, (t + 1) * P)
                nc.tensor.matmul(ps, xn_hi[:, rows], w_hi[:, g, :], start=True, stop=False)
                nc.tensor.matmul(ps, xn_hi[:, rows], w_lo[:, g, :], start=False, stop=False)
                nc.tensor.matmul(ps, xn_lo[:, rows], w_hi[:, g, :], start=False,
                                 stop=True).then_inc(scratch_full[u.bank], 1)

            def turn_heads(u, m, parity, j):
                pe.wait_ge(rotated_ready, m + 1)
                lo = NQK - P if j == 0 else (j - 1) * P
                turn4(u, lambda t: rotated[parity][:, t, lo:lo + P])

            def max_tile(m, slot, s, turned=()):
                if s % 8 == 0:
                    pe.wait_ge(hi_copied[s // 8], m * 16 + 16)
                    for u in turned:
                        read(pe, u)
                wait(pe, max_done, m * SLOTS + s - 1)
                nc.tensor.matmul(max_ps[s % 2][:], q_split[slot][:, s // NT, (s % NT) * P:(s % NT + 1) * P],
                                 k_hi[slot][:], start=True, stop=True).then_inc(max_full, 1)

            def max_row_turn(u, m, slot, part):
                pe.wait_ge(max_done, m * SLOTS + 8 * part + 8)
                nc.tensor.transpose(begin(u)[0:8, 0:P], neg_max[slot][:, 8 * part:8 * part + 8],
                                    ident[:]).then_inc(scratch_full[u.bank], 1)

            def score_tile(n, g, s):
                hd, c = s // NT, s % NT
                if c == 0 and hd % 2 == 0:
                    pe.wait_ge(max_placed, n * 32 + 16 + 8 * hd)
                wait(pe, exp_done, n * SLOTS + s - 1)
                keys = slice(c * P, (c + 1) * P)
                nc.tensor.matmul(score_ps[s % 2][:], k_hi[g][:, keys], q_split[g][:, hd, :], start=True, stop=False)
                nc.tensor.matmul(score_ps[s % 2][:], k_lo[g][0:65, keys], q_hi[g][0:65, hd, :], start=False,
                                 stop=True).then_inc(score_full, 1)

            def pv_tile(head, slot, hd, c):
                if c == 0:
                    pe.wait_ge(exp_done, head * NT + NT)
                    wait(pe, o_ready, head - 1)
                for kc in range(NT):
                    last = nc.tensor.matmul(pv_ps[hd % 2][:, c * 65:(c + 1) * 65],
                                            probs[hd % 2][:, kc, c * P:(c + 1) * P],
                                            raw[slot][:, kc, NQK:RAW], start=(kc == 0), stop=(kc == NT - 1))
                if c == NT - 1:
                    last.then_inc(pv_full, 1)

            def out_turn(u, heads, parity, pair):
                pe.wait_ge(o_ready, heads)
                turn4(u, lambda t: o_tok[parity][:, t, pair * P:(pair + 1) * P])

            def out_project(u, g, turned):
                for t in turned:
                    read(pe, t)
                ps = begin(u)
                for pair in range(2):
                    mm = nc.tensor.matmul(ps[:], w_o[:, 2 * g + pair, :], o_t[:, pair, :], start=(pair == 0),
                                          stop=(pair == 1))
                mm.then_inc(scratch_full[u.bank], 1)

            def keep_busy(count, ps):
                for _ in range(count):
                    nc.tensor.matmul(ps[:], w_hi[:, 0, 0:P], xn_hi[:], start=True, stop=True)

            pe.wait_ge(w_in, 16 * 4)
            turned = [pro["turn", 0, j] for j in range(3)]
            for use in PRO:
                u = pro[use]
                if use[0] == "xn_turn":
                    pe.wait_ge(xn_tok_ready, 1)
                    turn4(u, lambda t: x_tok[0][:, t, :])
                elif use[0] == "proj":
                    pe.wait_ge(xn_cur_ready, 1)
                    pe.wait_ge(w_lo_ready, use[1] + 1)
                    project(u, use[1], use[2])
                elif use[0] == "maxrow":
                    keep_busy(7, score_ps[0])
                    for s in range(8):
                        max_tile(0, 0, s, turned)
                        if s < 7:
                            keep_busy(1, score_ps[0])
                    keep_busy(2, score_ps[0])
                    max_row_turn(u, 0, 0, 0)
                    for s in range(8, 12):
                        max_tile(0, 0, s, turned)
                    keep_busy(3, score_ps[0])
                else:
                    if use[1:] == (0, 0):
                        pe.wait_ge(ffn_in, 16 * FFN_LOADS)
                        for i in range(2 * FB):
                            mm = nc.tensor.matmul(pv_ps[i // 4][:, i % 4 * D:(i % 4 + 1) * D], la[:, i, :],
                                                  lb[:, i, :], start=True, stop=True)
                        mm.then_inc(lora_ready, 1)
                    turn_heads(u, 0, 0, use[2])
            pe.wait_ge(w_o_in, 16)
            pe.wait_ge(w_lo_ready, KV)

            def body(kind, b):
                for g in range(GROUPS):
                    n = b * GROUPS + g
                    for s in range(SLOTS):
                        if kind == "first" and g == 0 and s == 1:
                            pe.wait_ge(w_ffn_ready, 1)
                        score_tile(n, g, s)
                        if kind == "first" and g == 0:
                            for m, tile in STEP_0_MAX.get(s, []):
                                max_tile(m, m, tile, [use_at(kind, b, 0, t)[2] for t in (0, 2, 3)] if m else turned)
                            keep_busy(STEP_0_BUSY.get(s, 0), pv_ps[1])
                        use = use_at(kind, b, g, s)
                        what, arg, u = use or (None, None, None)
                        if what == "proj":
                            pe.wait_ge(xn_cur_ready, b + (1 if g == 0 else 2))
                            project(u, (g + 3) % GROUPS, arg)
                        elif what == "turn":
                            turn_heads(u, n + 2, g % 2, arg)
                        elif what == "turn_1":
                            turn_heads(u, 1, 1, arg)
                        elif what == "maxrow" and arg == 1:
                            max_row_turn(u, n, g, 1)
                        elif what == "maxrow":
                            max_row_turn(u, n + 1, (g + 1) % GROUPS, 0)
                        elif what == "out_turn":
                            out_turn(u, n * HG, (g + 1) % 2, arg)
                        elif what == "out":
                            out_project(u, (g + 3) % GROUPS, [use_at(kind, b, g, t)[2] for t in (11, 12)])
                        elif what == "ffn1":
                            if g == 0:
                                pe.wait_ge(h0_ready, b + 1)
                                pe.wait_ge(w_ffn_ready, 1)
                            else:
                                read(pe, use_at(kind, b, g - 1, 14)[2])
                            ps = begin(u)
                            for t in range(NT):
                                mm = nc.tensor.matmul(ps[:, t * P:(t + 1) * P], h[g][:, t * P:(t + 1) * P],
                                                      w_ffn[:, 2 * g, :], start=True, stop=True)
                            mm.then_inc(scratch_full[u.bank], 1)
                        elif what == "xn_turn":
                            pe.wait_ge(xn_tok_ready, arg + 1)
                            turn4(u, lambda t: x_tok[arg][:, t, :])
                        elif what == "ffn_turn":
                            pe.wait_ge(f_norm, b * FB + g + 1)
                            turn4(u, lambda t: y_tok[:, t, :])
                        elif what == "ffn2":
                            read(pe, use_at(kind, b, g, 8)[2])
                            nc.tensor.matmul(begin(u)[:], w_ffn[:, 2 * g + 1, :], act_t, start=True,
                                             stop=True).then_inc(scratch_full[u.bank], 1)
                        elif what == "final":
                            read(pe, use_at(kind, b, 0, 13)[2])
                            turn4(u, lambda t: y_t[:, t * P:(t + 1) * P])
                        if not (kind == "first" and g == 0) and not (kind == "last" and g == 3):
                            max_tile(n + 1, (g + 1) % GROUPS, s)
                        hd = s // NT - 1
                        if hd >= 0:
                            pv_tile(n * HG + hd, g, hd, s % NT)
                        elif not (kind == "first" and g == 0):
                            pv_tile(n * HG - 1, (g + 3) % GROUPS, HG - 1, s % NT)

            batches(pe, body)

            out_turn(epi[0], B * H - 2, 1, 0)
            for c in range(NT):
                pv_tile(B * H - 1, 3, HG - 1, c)
            read(pe, epi[0])
            ps = begin(epi[2])
            nc.tensor.matmul(ps[:], w_o[:, H // 2 - 2, :], o_t[:, 0, :], start=True, stop=False)
            out_turn(epi[1], B * H, 1, 1)
            read(pe, epi[1])
            nc.tensor.matmul(ps[:], w_o[:, H // 2 - 1, :], o_t[:, 1, :], start=False,
                             stop=True).then_inc(scratch_full[epi[2].bank], 1)
            read(pe, epi[2])
            turn4(epi[3], lambda t: y_t[:, t * P:(t + 1) * P])

        @block.vector
        def _(dve):
            def x_stats(b):
                dve.wait_ge(x_in[b], 16)
                for t in range(b * NT, (b + 1) * NT):
                    last = nc.vector.bn_stats(ln_stats[:, t, :], x_tok[b][:, t - b * NT, :])
                last.then_inc(ln_stat, 1)

            def x_aggregate(b):
                dve.wait_ge(ln_stat, b + 1)
                for t in range(b * NT, (b + 1) * NT):
                    last = nc.vector.bn_aggr(ln_mv[:, t, :], ln_stats[:, t, :])
                return last

            def x_norm(b):
                dve.wait_ge(ln_rsdone, 1 if b == 0 else 2)
                for t in range(b * NT, (b + 1) * NT):
                    last = nc.vector.tensor_scalar(x_tok[b][:, t - b * NT, :], x_tok[b][:, t - b * NT, :], ln_mv[:, t, 0:1],
                                                   ln_rs[:, t:t + 1], ALU.subtract, ALU.mult)
                last.then_inc(xn_tok_ready, 1)

            def sum_squares(m, parity):
                dve.wait_ge(squared, m)
                nc.vector.tensor_reduce(ss[:], rotated[parity][:].rearrange("p t (j d) -> p (t j) d", d=DH), AX.X,
                                        ALU.add).then_inc(ss_ready, 1)

            def sum_squares_early():
                dve.wait_ge(early_squared, 1)
                nc.vector.tensor_reduce(early_ss[:], early_squares.rearrange("p t (j d) -> p (t j) d", d=DH), AX.X,
                                        ALU.add).then_inc(early_ss_ready, 1)

            def split(u, m, slot, j):
                ps = full(dve, u)
                dve.wait_ge(hi_ready, m * 6 + 2 * j + 2)
                if j == 0:
                    last = nc.vector.tensor_tensor(k_lo[slot][0:64, :], ps[64:128, :],
                                                   k_hi[slot][0:64, :].bitcast(F32), ALU.subtract)
                else:
                    for k in range(2):
                        head = 2 * j - 2 + k
                        last = nc.vector.tensor_tensor(q_split[slot][64:128, head, :], ps[64 * k:64 * k + 64, :],
                                                       q_hi[slot][0:64, head, :].bitcast(F32), ALU.subtract)
                last.then_inc(scratch_free[u.bank], 1)

            def reduce_max(m, slot, s):
                dve.wait_ge(max_full, m * SLOTS + s + 1)
                nc.vector.tensor_reduce(neg_max[slot][:, s:s + 1], max_ps[s % 2][:], AX.X, ALU.max,
                                        negate=True).then_inc(max_done, 1)

            def normalise(head, hd, parity):
                dve.wait_ge(pv_full, head + 1)
                pv = pv_ps[hd % 2][:, 0:NT * 65].rearrange("p (c d) -> p c d", d=65)
                nc.vector.reciprocal(inv_sum[hd % 2][:], pv[:, :, DH]).then_inc(inv_ready, 1)
                dve.wait_ge(inv_ready, head + 1)
                nc.vector.tensor_tensor(o_tok[parity][:, :, hd * DH:(hd + 1) * DH], pv[:, :, 0:DH],
                                        inv_sum[hd % 2][:].unsqueeze(2).to_broadcast([P, NT, DH]),
                                        ALU.mult).then_inc(o_ready, 1)

            def split_w(g):
                dve.wait_ge(w_hi_ready, g + 1)
                nc.vector.tensor_tensor(w_lo[:, g, :], w_qkv[:, g, :], w_hi[:, g, :].bitcast(F32),
                                        ALU.subtract).then_inc(w_lo_ready, 1)

            def split_xn(b, xn):
                dve.wait_ge(xn_hi_ready, b + 1)
                nc.vector.tensor_tensor(xn_lo[:], xn, xn_hi[:].bitcast(F32), ALU.subtract).then_inc(xn_cur_ready, 1)

            def add_out(u, before=None):
                if before:
                    read(dve, before)
                nc.vector.tensor_tensor(y_t[:], full(dve, u)[:], y_t[:], ALU.add).then_inc(scratch_free[u.bank], 1)

            def final_rows(u, b):
                dve.wait_ge(x_again, b * 16)
                rows = out_tok[:].rearrange("p t d -> p (t d)")
                nc.vector.tensor_tensor(rows, full(dve, u)[:], rows, ALU.add).then_inc(scratch_free[u.bank], 1)

            def rotate_0():
                r, dst = raw[0], rotated[0]
                nc.vector.tensor_tensor(dst[:], r[:, :, 0:NQK], cos_w[:], ALU.mult)
                for s in range(2):
                    last = nc.vector.tensor_tensor(
                        halves(early_crossed)[:, :, :, s, :], halves(r[:, :, 0:NQK])[:, :, :, 1 - s, :],
                        halves(sin_w[:])[:, :, :, s, :], ALU.mult)
                last.then_inc(dve_step, 1)
                dve.wait_ge(dve_step, 1)
                nc.vector.tensor_tensor(dst[:], dst[:], early_crossed, ALU.add).then_inc(dve_step, 1)
                dve.wait_ge(dve_step, 2)
                dve.wait_ge(early_rms, 2)
                d3 = dst[:].rearrange("p t (j d) -> p (t j) d", d=DH)
                nc.vector.tensor_tensor(d3, d3, early_rs[:].unsqueeze(2).to_broadcast([P, NT * NV, DH]),
                                        ALU.mult).then_inc(rotated_ready, 1)

            for i in range(GROUPS):
                nc.vector.memset(k_lo[i][64:65, :].bitcast(F32), 1.0)
            x_stats(0)
            x_aggregate(0).then_inc(ln_agg, 1)
            x_norm(0)
            split_w(0)
            read(dve, pro["xn_turn", 0])
            split_xn(0, xn_t[:, 0:L])
            for g in range(1, KV):
                split_w(g)
            dve.wait_ge(tab_in, 16 * 8)
            for t in range(NT):
                for dst, tab, w in ((cos_w, cos_sb, w_rep), (sin_w, sin_sb, w_swap)):
                    nc.vector.tensor_tensor(dst[:, t, :].rearrange("p (j d) -> p j d", d=DH), w,
                                            tab[:, t, :].unsqueeze(1).to_broadcast([P, NV, DH]),
                                            ALU.mult).then_inc(tables_set, 1)
            sum_squares_early()
            for u in (pro["proj", 0, NT - 2], pro["proj", 0, NT - 1]):
                read(dve, u)
            dve.wait_ge(tables_set, 2 * NT)
            rotate_0()
            sum_squares(1, 1)
            dve.wait_ge(ffn_in, 16 * FFN_LOADS)
            nc.vector.tensor_scalar(deq_w, q_int, 1.0 / 7.5, -1.0, ALU.mult, ALU.add).then_inc(deq, 1)
            dve.wait_ge(deq, 1)
            nc.vector.tensor_tensor(deq_w, deq_w, scale_rep, ALU.mult).then_inc(deq, 1)
            for j in range(3):
                split(pro["turn", 0, j], 0, 0, j)
                if j == 0:
                    dve.wait_ge(deq, 2)
                    dve.wait_ge(lora_ready, 1)
                    w_flat = w_ffn[:].rearrange("p i o -> p (i o)")
                    nc.vector.tensor_tensor(w_flat[:, 0:4 * D], deq_w[:, 0:4 * D], pv_ps[0][:], ALU.add)
                    nc.vector.tensor_tensor(w_flat[:, 4 * D:6 * D], deq_w[:, 4 * D:6 * D], pv_ps[1][:, 0:2 * D],
                                            ALU.add).then_inc(w_ffn_ready, 1)
            for s in range(8):
                reduce_max(0, 0, s)
            for s in range(8, 12):
                reduce_max(0, 0, s)
            nc.vector.tensor_copy(h[0], xn_t[:, 0:L]).then_inc(h0_ready, 1)

            def body(kind, b):
                for g in range(GROUPS):
                    n = b * GROUPS + g
                    for s in range(SLOTS):
                        if s % NT == 0 and not (kind == "first" and g == 0 and s < 8):
                            hd = s // NT - 2
                            normalise(n * HG + hd, hd % HG, g % 2 if hd >= 0 else (g + 1) % 2)
                        if g == 0 and s == 0 and kind != "first":
                            nc.vector.tensor_copy(h[0], xn_t[:, bass.ds(b * L, L)] if kind == "mid" else
                                                  xn_t[:, b * L:(b + 1) * L]).then_inc(h0_ready, 1)
                        if g == 1 and s == 0 and kind != "last":
                            split_xn(b + 1, xn_t[:, bass.ds((b + 1) * L, L)] if kind == "mid" else xn_t[:, L:2 * L])
                        if kind == "first" and g == 0:
                            for m, tile in STEP_0_MAX.get(s, []):
                                reduce_max(m, m, tile)
                            if s == 0:
                                sum_squares(2, 0)
                        if kind == "first" and g == 0 and s in (5, 6, 7):
                            x_stats(s - 4)
                            last = x_aggregate(s - 4)
                            if s == 7:
                                last.then_inc(ln_agg, 1)
                        if kind == "first" and s == 13 and g < B - 1:
                            x_norm(g + 1)
                        if g < FB and s == 4:
                            dve.wait_ge(f_rsdone, b * FB + g + 1)
                            for t in range(NT):
                                last = nc.vector.tensor_scalar(y_tok[:, t, :], y_tok[:, t, :], f_mv[:, t, 0:1],
                                                               f_rs[:, t:t + 1], ALU.subtract, ALU.mult)
                            last.then_inc(f_norm, 1)
                        if s == 10 and use_at(kind, b, g, 7):
                            sum_squares(n + 3, (g + 3) % 2)
                        what, arg, u = use_at(kind, b, g, s) or (None, None, None)
                        if what == "turn":
                            split(u, n + 2, (g + 2) % GROUPS, arg)
                        elif what == "turn_1":
                            split(u, 1, 1, arg)
                        elif what == "ffn1":
                            k = b * FB + g + 1
                            nc.vector.tensor_tensor(y_tok[:], full(dve, u)[:].rearrange("p (t d) -> p t d", d=D),
                                                    bias_row[:, g, :].unsqueeze(1).to_broadcast([P, NT, D]),
                                                    ALU.add).then_inc(scratch_free[u.bank], 1)
                            read(dve, u)
                            for t in range(NT):
                                last = nc.vector.bn_stats(f_stats[:, t, :], y_tok[:, t, :])
                            last.then_inc(f_stat, 1)
                        elif what == "ffn2":
                            nc.vector.scalar_tensor_tensor(
                                out=h[g + 1], in0=full(dve, u)[:], scalar=bias_col[:, 2 * g + 1:2 * g + 2],
                                in1=h[g], op0=ALU.add, op1=ALU.add).then_inc(scratch_free[u.bank], 1)
                        elif what == "final":
                            final_rows(u, b)
                        elif what == "out" and g == 2:
                            add_out(u, use_at(kind, b, 1, 13)[2])
                        elif what == "out" and g == 3:
                            dve.wait_ge(streams_joined, b + 1)
                            add_out(u)
                        elif what == "out" and g == 0:
                            add_out(u, out_before(kind, b))
                        if g == 2 and s == 15:
                            read(dve, use_at(kind, b, 2, 13)[2])
                            read(dve, use_at(kind, b, 2, 14)[2])
                            nc.vector.tensor_tensor(y_t[:], y_t[:], h[FB], ALU.add).then_inc(streams_joined, 1)
                        if what == "ffn1":
                            dve.wait_ge(f_stat, k)
                        if not (kind == "first" and g == 0) and not (kind == "last" and g == 3):
                            reduce_max(n + 1, (g + 1) % GROUPS, s)
                        if what == "ffn1":
                            for t in range(NT):
                                last = nc.vector.bn_aggr(f_mv[:, t, :], f_stats[:, t, :])
                            last.then_inc(f_agg, 1)

            batches(dve, body)
            for head in (B * H - 2, B * H - 1):
                normalise(head, head % HG, 1)
            add_out(epi[2])
            final_rows(epi[3], B)


def kernel(**inputs):
    import concourse.bacc as bacc
    from concourse.bass_utils import run_bass_kernel_spmd

    given = {name.replace("L0_", ""): np.asarray(a) for name, a in inputs.items()}
    t = np.ascontiguousarray

    inv_freq = (1.0 / 10000.0 ** (np.arange(0, DH, 2, dtype=np.float32) / DH)).astype(np.float32)
    freqs = np.arange(L - 1, dtype=np.float32)[:, None] * inv_freq[None, :]
    cos, sin = np.ones((L, DH), np.float32), np.zeros((L, DH), np.float32)
    cos[1:] = np.cos(np.concatenate([freqs, freqs], 1))
    sin[1:] = np.concatenate([-np.sin(freqs), np.sin(freqs)], 1)

    arrays = {
        "x": t(given["attn_inputs"]),
        "wq": t(given["attn_Wq"].T), "wk": t(given["attn_Wk"].T), "wv": t(given["attn_Wv"].T),
        "wo": t(given["attn_Wo"].T),
        "q_w": t(given["attn_q_norm_w"]), "k_w": t(given["attn_k_norm_w"]),
        "qweights": t(given["ffn_qweights"].transpose(0, 2, 1)), "scales": t(given["ffn_scales"].transpose(0, 2, 1)),
        "biases": t(given["ffn_biases"]), "biases_t": t(given["ffn_biases"].T),
        "lora_a": t(given["ffn_lora_a"]), "lora_b_t": t(given["ffn_lora_b"].transpose(0, 2, 1)),
        "gamma_t": t(given["ffn_ln_gamma"].T), "beta_t": t(given["ffn_ln_beta"].T),
        "cos": cos * np.float32(DH ** 0.5), "sin": sin * np.float32(DH ** 0.5), "identity": np.eye(P, dtype=np.float32),
    }
    nc = bacc.Bacc("TRN2", target_bir_lowering=False, num_devices=1)
    aps = {name: nc.dram_tensor(name, a.shape, mybir.dt.from_np(a.dtype), kind="ExternalInput").ap()
           for name, a in arrays.items()}
    out = nc.dram_tensor("out", (B, L, D), F32, kind="ExternalOutput").ap()
    attention_ffn(nc, out=out, **aps)
    result = run_bass_kernel_spmd(nc, [arrays], core_ids=[0])
    return result.results[0]["out"]
```
